# Optimizing a Trainium2 kernel written in Bass

```python
import numpy as np
import jax
import jax.numpy as jnp

def _softmax(x, axis=-1):
    return jax.nn.softmax(x, axis=axis)
def _gelu(x):
    return jax.nn.gelu(x, approximate=True)
def _silu(x):
    return jax.nn.silu(x)
def _sigmoid(x):
    return jax.nn.sigmoid(x)
def _layernorm(x, axis=-1, eps=1e-5):
    m = jnp.mean(x, axis=axis, keepdims=True)
    v = jnp.var(x, axis=axis, keepdims=True)
    return (x - m) / jnp.sqrt(v + eps)
def _scatter_add(tgt, idx, src, axis=0):
    return tgt.at[idx].add(src)
def _segment_sum(src, seg, n):
    return jax.ops.segment_sum(src, seg, n)

kernel_name = 'mk_adj_preln_d4_adj_64_6379af'

def setup_inputs(seed: int = 0):
    np.random.seed(seed)
    _w = jnp.asarray
    def _rec_inputs():
        import jax
        import jax.numpy as jnp
        _gk = jax.random.key(seed)
        x = -0.006082 + 1.001 * jax.random.normal(jax.random.fold_in(_gk, 1), (128, 128, 64), jnp.float32)
        _a = jax.random.bernoulli(jax.random.fold_in(_gk, 2), 0.0625, (128, 128, 128))
        _a = jnp.logical_or(_a, jnp.swapaxes(_a, -1, -2))
        _a = jnp.logical_or(_a, jnp.eye(128, dtype=bool))
        _af = _a.astype(jnp.float32)
        _af = _af * jax.random.uniform(jax.random.fold_in(_gk, 3), (128, 128, 128), jnp.float32, 0.05, 4.42607)
        adj = _af
        _nm = jnp.ones((128, 128), dtype=bool)
        nodemask = jnp.where(_nm, 1.0, 0.0).astype(jnp.float32)
        return x, adj, nodemask
    x, adj, nodemask = _rec_inputs()
    def _L0_gnn_setup():
        import jax, jax.numpy as jnp
        import numpy as np
        key = jax.random.key(seed)
        ks = jax.random.split(key, 6)
        B, N, F, H, O = (2, 512, 64, 192, 64)
        x = jax.random.normal(ks[0], (B, N, F), dtype=jnp.float32)
        adj = jax.random.normal(ks[1], (B, N, N), dtype=jnp.float32)
        W1 = jax.random.normal(ks[2], (2 * F, H), dtype=jnp.float32) * (1.0 / np.sqrt(2 * F))
        b1 = jax.random.normal(ks[3], (H,), dtype=jnp.float32) * 0.02
        W2 = jax.random.normal(ks[4], (H, O), dtype=jnp.float32) * (1.0 / np.sqrt(H))
        b2 = jax.random.normal(ks[5], (O,), dtype=jnp.float32) * 0.02
        return {'x': x, 'adj': adj, 'W1': W1, 'b1': b1, 'W2': W2, 'b2': b2}
    _L0_gnn_all = _L0_gnn_setup()
    _L0_gnn_in = {k: v for k, v in _L0_gnn_all.items() if k in ('W1', 'b1', 'W2', 'b2', )}
    del _L0_gnn_all

    def _L1_gnn_setup():
        import jax, jax.numpy as jnp
        import numpy as np
        NORM = 1.0

        def _glorot(key, shape):
            fan_in, fan_out = shape
            lim = float(np.sqrt(6.0 / (fan_in + fan_out)))
            return jax.random.uniform(key, shape, jnp.float32, -lim, lim)

        def _gcn_layer(h, adj, W, b):
            msg = h @ W + b
            agg = jnp.einsum('bij,bjd->bid', adj, msg) / NORM
            return jax.nn.relu(agg)
        key = jax.random.key(seed)
        ks = jax.random.split(key, 12)
        B, N = (8, 2048)
        latent, hidden, out_dim = (64, 128, 64)
        inp = {'latent_features': jax.random.normal(ks[0], (B, N, latent), jnp.float32), 'adjacency_matrix': jax.random.uniform(ks[1], (B, N, N), jnp.float32), 'node_mask': jnp.ones((B, N, 1), jnp.float32), 'W0': _glorot(ks[2], (latent, hidden)), 'b0': jnp.zeros((hidden,), jnp.float32), 'W1': _glorot(ks[3], (hidden, hidden)), 'b1': jnp.zeros((hidden,), jnp.float32), 'W2': _glorot(ks[4], (hidden, hidden)), 'b2': jnp.zeros((hidden,), jnp.float32), 'Wout': _glorot(ks[5], (hidden, out_dim)), 'bout': jnp.zeros((out_dim,), jnp.float32)}
        return inp
    _L1_gnn_all = _L1_gnn_setup()
    _L1_gnn_in = {k: v for k, v in _L1_gnn_all.items() if k in ('W0', 'b0', 'W1', 'b1', 'W2', 'b2', 'Wout', 'bout', )}
    del _L1_gnn_all

    def _L2_gnn_setup():
        import jax, jax.numpy as jnp
        import numpy as np
        B, N, D_IN, D_OUT = (16, 2048, 64, 64)
        BN_EPS = 1e-05
        key = jax.random.key(seed)
        k_x, k_adj, k_len, k_w = jax.random.split(key, 4)
        x = jax.random.normal(k_x, (B, N, D_IN), dtype=jnp.float32)
        adj_matrix = jax.random.uniform(k_adj, (B, N, N), dtype=jnp.float32)
        lengths = jax.random.randint(k_len, (B,), N // 2, N + 1)
        mask = (jnp.arange(N)[None, :] < lengths[:, None]).astype(jnp.float32)
        weight = jax.random.normal(k_w, (D_IN, D_OUT), dtype=jnp.float32) * np.sqrt(2.0 / (D_IN + D_OUT))
        bias = jnp.zeros((D_OUT,), dtype=jnp.float32)
        gamma = jnp.ones((D_OUT,), dtype=jnp.float32)
        beta = jnp.zeros((D_OUT,), dtype=jnp.float32)
        return {'x': x, 'adj_matrix': adj_matrix, 'mask': mask, 'weight': weight, 'bias': bias, 'gamma': gamma, 'beta': beta}
    _L2_gnn_all = _L2_gnn_setup()
    _L2_gnn_in = {k: v for k, v in _L2_gnn_all.items() if k in ('weight', 'bias', 'gamma', 'beta', )}
    del _L2_gnn_all

    def _L3_gnn_setup():
        import jax, jax.numpy as jnp
        import numpy as np
        B, N, H = (4, 512, 64)
        key = jax.random.key(seed)
        ks = jax.random.split(key, 11)
        s = 0.05
        return {'t': jnp.float32(0.5), 'h': jax.random.normal(ks[0], (B, N, H), dtype=jnp.float32), 'adjacency': jax.random.uniform(ks[1], (B, N, N), dtype=jnp.float32), 'W1': jax.random.normal(ks[2], (2 * H, H), dtype=jnp.float32) * s, 'b1': jax.random.normal(ks[3], (H,), dtype=jnp.float32) * s, 'W2': jax.random.normal(ks[4], (H, H), dtype=jnp.float32) * s, 'b2': jax.random.normal(ks[5], (H,), dtype=jnp.float32) * s, 'E1': jax.random.normal(ks[6], (2 * H, H), dtype=jnp.float32) * s, 'be1': jax.random.normal(ks[7], (H,), dtype=jnp.float32) * s, 'E2': jax.random.normal(ks[8], (H, 1), dtype=jnp.float32) * s, 'be2': jax.random.normal(ks[9], (1,), dtype=jnp.float32) * s}
    _L3_gnn_all = _L3_gnn_setup()
    _L3_gnn_in = {k: v for k, v in _L3_gnn_all.items() if k in ('t', 'W1', 'b1', 'W2', 'b2', 'E1', 'be1', 'E2', 'be2', )}
    del _L3_gnn_all

    return {
        "x": x,
        "adj": adj,
        "nodemask": nodemask,
        "L0_gnn_W1": _L0_gnn_in["W1"],
        "L0_gnn_b1": _L0_gnn_in["b1"],
        "L0_gnn_W2": _L0_gnn_in["W2"],
        "L0_gnn_b2": _L0_gnn_in["b2"],
        "L1_gnn_W0": _L1_gnn_in["W0"],
        "L1_gnn_b0": _L1_gnn_in["b0"],
        "L1_gnn_W1": _L1_gnn_in["W1"],
        "L1_gnn_b1": _L1_gnn_in["b1"],
        "L1_gnn_W2": _L1_gnn_in["W2"],
        "L1_gnn_b2": _L1_gnn_in["b2"],
        "L1_gnn_Wout": _L1_gnn_in["Wout"],
        "L1_gnn_bout": _L1_gnn_in["bout"],
        "L2_gnn_weight": _L2_gnn_in["weight"],
        "L2_gnn_bias": _L2_gnn_in["bias"],
        "L2_gnn_gamma": _L2_gnn_in["gamma"],
        "L2_gnn_beta": _L2_gnn_in["beta"],
        "L3_gnn_t": _L3_gnn_in["t"],
        "L3_gnn_W1": _L3_gnn_in["W1"],
        "L3_gnn_b1": _L3_gnn_in["b1"],
        "L3_gnn_W2": _L3_gnn_in["W2"],
        "L3_gnn_b2": _L3_gnn_in["b2"],
        "L3_gnn_E1": _L3_gnn_in["E1"],
        "L3_gnn_be1": _L3_gnn_in["be1"],
        "L3_gnn_E2": _L3_gnn_in["E2"],
        "L3_gnn_be2": _L3_gnn_in["be2"],
    }

def reference(x, adj, nodemask, L0_gnn_W1, L0_gnn_b1, L0_gnn_W2, L0_gnn_b2, L1_gnn_W0, L1_gnn_b0, L1_gnn_W1, L1_gnn_b1, L1_gnn_W2, L1_gnn_b2, L1_gnn_Wout, L1_gnn_bout, L2_gnn_weight, L2_gnn_bias, L2_gnn_gamma, L2_gnn_beta, L3_gnn_t, L3_gnn_W1, L3_gnn_b1, L3_gnn_W2, L3_gnn_b2, L3_gnn_E1, L3_gnn_be1, L3_gnn_E2, L3_gnn_be2):
    import jax
    import jax.numpy as jnp
    def _L0_gnn_ref(x, adj, W1, b1, W2, b2):
        import jax, jax.numpy as jnp
        import numpy as np
        F = x.shape[-1]
        mask = (adj > 0.0).astype(x.dtype)
        W1a, W1b = (W1[:F], W1[F:])
        xj_proj = x @ W1a
        diff = x[:, :, None, :] - x[:, None, :, :]
        h = jax.nn.relu(xj_proj[:, :, None, :] + diff @ W1b + b1)
        hm = jnp.einsum('bjkh,bjk->bjh', h, mask)
        deg = jnp.sum(mask, axis=-1)
        return hm @ W2 + deg[..., None] * b2

    def _L1_gnn_ref(latent_features, adjacency_matrix, node_mask, W0, b0, W1, b1, W2, b2, Wout, bout):
        import jax, jax.numpy as jnp
        import numpy as np
        NORM = 1.0

        def _glorot(key, shape):
            fan_in, fan_out = shape
            lim = float(np.sqrt(6.0 / (fan_in + fan_out)))
            return jax.random.uniform(key, shape, jnp.float32, -lim, lim)

        def _gcn_layer(h, adj, W, b):
            msg = h @ W + b
            agg = jnp.einsum('bij,bjd->bid', adj, msg) / NORM
            return jax.nn.relu(agg)
        h = _gcn_layer(latent_features, adjacency_matrix, W0, b0)
        h = _gcn_layer(h, adjacency_matrix, W1, b1)
        h = _gcn_layer(h, adjacency_matrix, W2, b2)
        return (h @ Wout + bout) * node_mask

    def _L2_gnn_ref(x, adj_matrix, mask, weight, bias, gamma, beta):
        import jax, jax.numpy as jnp
        import numpy as np
        B, N, D_IN, D_OUT = (16, 2048, 64, 64)
        BN_EPS = 1e-05
        y = jnp.matmul(adj_matrix, x) + x
        y = jnp.matmul(y, weight) + bias
        norm = jnp.linalg.norm(y, axis=2, keepdims=True)
        y = y / jnp.maximum(norm, 1e-12)
        m = mask[..., None]
        cnt = jnp.sum(mask)
        mean = jnp.sum(y * m, axis=(0, 1)) / cnt
        var = jnp.sum((y - mean) ** 2 * m, axis=(0, 1)) / cnt
        y = ((y - mean) / jnp.sqrt(var + BN_EPS) * gamma + beta) * m
        return jax.nn.relu(y)

    def _L3_gnn_ref(t, h, adjacency, W1, b1, W2, b2, E1, be1, E2, be2):
        import jax, jax.numpy as jnp
        import numpy as np
        B, N, H = (4, 512, 64)
        messages = jnp.einsum('bij,bjh->bih', adjacency, h)
        node_in = jnp.concatenate([h, messages], axis=-1)
        dh = jnp.tanh(node_in @ W1 + b1) @ W2 + b2
        hd = h.shape[-1]
        pi = h @ E1[:hd]
        pj = h @ E1[hd:]
        eh = jnp.tanh(pi[:, :, None, :] + pj[:, None, :, :] + be1)
        edge_updates = (eh @ E2)[..., 0] + be2[0]
        _ = adjacency + edge_updates
        return dh

    h = jnp.maximum(_layernorm(x, axis=-1), 0.0)
    x = x + _L0_gnn_ref(h, adj, L0_gnn_W1, L0_gnn_b1, L0_gnn_W2, L0_gnn_b2)
    h = jnp.maximum(_layernorm(x, axis=-1), 0.0)
    x = x + _L1_gnn_ref(h, adj, nodemask[..., None], L1_gnn_W0, L1_gnn_b0, L1_gnn_W1, L1_gnn_b1, L1_gnn_W2, L1_gnn_b2, L1_gnn_Wout, L1_gnn_bout)
    h = jnp.maximum(_layernorm(x, axis=-1), 0.0)
    x = x + _L2_gnn_ref(h, adj, nodemask, L2_gnn_weight, L2_gnn_bias, L2_gnn_gamma, L2_gnn_beta)
    h = jnp.maximum(_layernorm(x, axis=-1), 0.0)
    x = x + _L3_gnn_ref(L3_gnn_t, h, adj, L3_gnn_W1, L3_gnn_b1, L3_gnn_W2, L3_gnn_b2, L3_gnn_E1, L3_gnn_be1, L3_gnn_E2, L3_gnn_be2)
    return x


_drawn_inputs = setup_inputs


def setup_inputs(seed=0):
    import zlib

    import numpy as np

    out = dict(_drawn_inputs(seed))
    spreads = {'L1_gnn_b0': (0.0, 0.1),
     'L1_gnn_b1': (0.0, 0.755),
     'L1_gnn_b2': (0.0, 0.8),
     'L1_gnn_bout': (0.0, 0.8),
     'L2_gnn_bias': (0.0, 0.8),
     'L2_gnn_gamma': (1.0, 0.6),
     'L2_gnn_beta': (0.0, 0.8)}
    factors = {'L0_gnn_b1': 3.298,
     'L2_gnn_weight': 8.0,
     'L3_gnn_W1': 8.0,
     'L3_gnn_b1': 8.0,
     'L3_gnn_W2': 8.0,
     'L3_gnn_b2': 8.0}
    for name, (base, spread) in spreads.items():
        noise = np.random.default_rng([zlib.crc32(name.encode()), seed]).standard_normal(out[name].shape)
        drawn = base * np.exp(spread * noise) if base else spread * noise
        out[name] = jnp.asarray(drawn.astype(out[name].dtype))
    for name, factor in factors.items():
        out[name] = (out[name] * factor).astype(out[name].dtype)
    return out
```

```python
import concourse.bass as bass
from concourse import mybir
from contextlib import ExitStack

F32 = mybir.dt.float32
F16 = mybir.dt.float16
I32 = mybir.dt.int32
ALU = mybir.AluOpType
ACT = mybir.ActivationFunctionType
AX = mybir.AxisListType


def gnn_stack_kernel(nc, a, out):
    B, N, F = a["x"].shape
    H = a["L0_gnn_W2"].shape[0]
    D1 = a["L1_gnn_W0"].shape[1]
    GS = 4
    NG = B // GS
    NI = NG // 2
    SC = 4
    EPS = 1e-5
    KEY = 257.0
    XC = 512
    NXC = B * F // XC
    GX = XC // F

    ctx = ExitStack()
    with ctx:
        def sb(name, shape, dt=F32):
            return ctx.enter_context(nc.sbuf_tensor(name, shape, dt))

        def sem(name):
            return ctx.enter_context(nc.semaphore(name))

        x = sb("x_all", [N, B * F])
        adjT = sb("adjT_all", [N, B * N])
        ident = sb("ident", [N, N])
        ident16 = sb("ident16", [N, N], F16)
        rankw = sb("rankw", [N, N], F16)
        ones16 = sb("ones16", [N, N], F16)
        ones = sb("ones", [N, N])
        key_i = sb("key_i", [N, N // SC + 1], I32)
        slot_key = sb("slot_key", [N, N // SC + 1])
        eps_col = sb("eps_col", [N, 1])
        w1a = sb("w1a", [F, H])
        w1b = sb("w1b", [F, H])
        wac = sb("wac", [F + 1, 2 * H])
        wmax = sb("wmax", [N, 1])
        wmax_all = sb("wmax_all", [N, 1])
        wexp = sb("wexp", [N, 1])
        wscale = sb("wscale", [N, 1])
        unscale = sb("unscale", [N, 1])
        w2a = sb("w2a", [N, F])
        w2b = sb("w2b", [H - N + 1, F])
        l1w0 = sb("l1w0", [F + 1, D1])
        l1w1 = sb("l1w1", [D1, D1])
        l1w2 = sb("l1w2", [D1, D1])
        l1wo = sb("l1wo", [D1, F])
        l1b1 = sb("l1b1", [N, D1])
        l1b2 = sb("l1b2", [N, D1])
        l1bo = sb("l1bo", [N, F])
        l2w = sb("l2w", [F + 1, F])
        gamma = sb("gamma", [N, F])
        beta = sb("beta", [N, F])
        l3w1 = sb("l3w1", [2 * F, F])
        l3b1 = sb("l3b1", [F, 1])
        l3w2 = sb("l3w2", [F + 1, F])
        nm_in = sb("nm_in", [B, N])
        nm = sb("nm", [N, B])
        rcnt = sb("rcnt", [N, 1])
        cnt_col = sb("cnt_col", [N, 1])
        bn6 = sb("bn6", [N, B, 6])
        var = sb("var", [N, B])
        dif = sb("dif", [N, B])
        msum = sb("msum", [N, B])
        std = sb("std", [N, B])
        rstd = sb("rstd", [N, B])
        nmr = sb("nmr", [N, B])
        adj_in = sb("adj_in", [N, 2, GS * N])
        sgn = sb("sgn", [N, GS * N], F16)
        mask = sb("mask", [N, 2, GS * N], F16)
        rs = sb("rs", [N, 2, GS, SC, N], F16)
        onehot = sb("onehot", [N, (N // SC) * SC * N], F16)
        y = onehot[:, :].bitcast(F32)
        maxdeg = sb("maxdeg", [1, GS])
        maxdeg_i = sb("maxdeg_i", [1, GS], I32)
        chunks = sb("chunks", [1, B], I32)
        neg_slots = sb("neg_slots", [1, GS], F16)
        neg_pad = sb("neg_pad", [N, 2, GS])
        h0 = sb("h0", [N, GS * F])
        hT0 = sb("hT0", [F + 1, 2, GS * N])
        ac32 = sb("ac32", [N, 2, 2 * H])
        ac_hi = sb("ac_hi", [N, 4, 2 * H], F16)
        ac_lo = sb("ac_lo", [N, 4, 2 * H], F16)
        acc = sb("acc", [N, 4, 2 * H])
        hm = sb("hm", [N, 2, H])
        hmTa = sb("hmTa", [N, 2, N])
        hmTb = sb("hmTb", [H - N + 1, 2, GS * N])
        hn = sb("hn", [N, 2, (GS + 1) * F])
        hT = hT0
        msg = adj_in
        hid = sb("hid", [N, 2, GS * N])
        upd = sb("upd", [N, 2, GS * F])
        ss = sb("ss", [N, B])
        tmp = rs[:, :, :, :, :].bitcast(F32).rearrange("p u q t j -> p (u q t j)")\
            .rearrange("p (a c) -> p a c", c=XC)
        stat = sb("stat", [N, 6, F])

        bank = [ctx.enter_context(nc.psum_tensor(f"bank{n}", [N, 512], F32)) for n in range(8)]

        adj_v = a["adj"].rearrange("b i j -> i b j")
        x_v = a["x"].rearrange("b n f -> n b f")
        out_v = out.rearrange("b n f -> n b f")
        x3 = x[:, :].rearrange("p (b f) -> p b f", f=F)
        ds = bass.ds

        s_w = sem("weights_loaded")
        s_x = [sem(f"x_loaded{n}") for n in range(4)]
        s_adj = [sem(f"adj_loaded{p}") for p in range(2)]
        s_const = sem("constants_made")
        s_pstep = sem("pool_setup_step")
        s_vstep = sem("vector_setup_step")
        s_wmax = sem("weight_max_ready")
        s_wall = sem("weight_max_spread")
        s_nmT = sem("nodemask_transposed")
        s_nm = sem("nodemask_copied")
        s_cnt = sem("nodemask_counted")
        s_bn = sem("layernorm_stats_made")
        s_lnstep = sem("layernorm_step")
        s_var64 = sem("variances_ready")
        s_std = sem("std_ready")
        s_rstd = sem("rstd_ready")
        s_ln = sem("layernorm_scales_ready")

        def row(ap, n):
            return ap.rearrange("(a n) -> a n", a=1)

        def spread(ap, n):
            return ap.unsqueeze(0).broadcast_to([N, n])

        loads = [
            (w1a[:, :], a["L0_gnn_W1"][0:F, :]), (w1b[:, :], a["L0_gnn_W1"][F:2 * F, :]),
            (wac[F:F + 1, 0:H], row(a["L0_gnn_b1"], H)),
            (w2a[:, :], a["L0_gnn_W2"][0:N, :]), (w2b[0:H - N, :], a["L0_gnn_W2"][N:H, :]),
            (w2b[H - N:H - N + 1, :], row(a["L0_gnn_b2"], F)),
            (l1w0[0:F, :], a["L1_gnn_W0"]), (l1w0[F:F + 1, :], row(a["L1_gnn_b0"], D1)),
            (l1w1[:, :], a["L1_gnn_W1"]), (l1w2[:, :], a["L1_gnn_W2"]), (l1wo[:, :], a["L1_gnn_Wout"]),
            (l1b1[:, :], spread(a["L1_gnn_b1"], D1)), (l1b2[:, :], spread(a["L1_gnn_b2"], D1)),
            (l1bo[:, :], spread(a["L1_gnn_bout"], F)),
            (l2w[0:F, :], a["L2_gnn_weight"]), (l2w[F:F + 1, :], row(a["L2_gnn_bias"], F)),
            (gamma[:, :], spread(a["L2_gnn_gamma"], F)), (beta[:, :], spread(a["L2_gnn_beta"], F)),
            (l3w1[:, :], a["L3_gnn_W1"]), (l3b1[:, :], a["L3_gnn_b1"].rearrange("(n a) -> n a", a=1)),
            (l3w2[0:F, :], a["L3_gnn_W2"]), (l3w2[F:F + 1, :], row(a["L3_gnn_b2"], F)),
            (nm_in[:, :], a["nodemask"]),
        ]
        ALL_W = 16 * len(loads)

        def load_adj(eng, g, p):
            eng.dma_start(adj_in[:, p, :].rearrange("i (b j) -> i b j", j=N), adj_v[:, ds(GS * g, GS), :])\
               .then_inc(s_adj[p], 16)

        def layernorm_std(act, n):
            act.wait_ge(s_var64, n)
            nc.scalar.activation(std[:, :], var[:, :], ACT.Sqrt, bias=eps_col[:, 0:1], scale=1.0 / F)\
              .then_inc(s_std, 1)

        def layernorm_scales(dve, n):
            v = nc.vector
            m0, q0, m1, q1 = (bn6[:, :, k] for k in (1, 2, 4, 5))
            v.tensor_tensor(msum[:, :], m0, m1, ALU.add)
            v.tensor_tensor(dif[:, :], m0, m1, ALU.subtract)
            v.tensor_tensor(var[:, :], q0, q1, ALU.add).then_inc(s_lnstep, 1)
            dve.wait_ge(s_lnstep, 2 * n - 1)
            v.scalar_tensor_tensor(out=dif[:, :], in0=dif[:, :], scalar=F / 4.0, in1=dif[:, :],
                                   op0=ALU.mult, op1=ALU.mult).then_inc(s_lnstep, 1)
            dve.wait_ge(s_lnstep, 2 * n)
            v.tensor_tensor(var[:, :], var[:, :], dif[:, :], ALU.add).then_inc(s_var64, 1)
            dve.wait_ge(s_std, n)
            v.reciprocal(rstd[:, :], std[:, :]).then_inc(s_rstd, 1)
            dve.wait_ge(s_rstd, n)
            v.scalar_tensor_tensor(out=nmr[:, :], in0=msum[:, :], scalar=-0.5, in1=rstd[:, :],
                                   op0=ALU.mult, op1=ALU.mult).then_inc(s_ln, 1)

        def stats(b):
            return nc.vector.bn_stats(bn6[:, ds(b, 1), :].rearrange("p a t -> p (a t)"), x[:, ds(b * F, F)])

        with nc.Block() as block:
            @block.sync
            def _(sp):
                load_adj(sp, 0, 0)
                for n in range(4):
                    sp.dma_start(x3[:, 32 * n:32 * n + 32, :], x_v[:, 32 * n:32 * n + 32, :]).then_inc(s_x[n], 16)
                load_adj(sp, 1, 1)

            @block.gpsimd
            def _(pool):
                g = nc.gpsimd
                g.memset(ident[:, :], 0.0)
                g.memset(ident16[:, :], 0.0)
                g.memset(rankw[:, :], 1.0).then_inc(s_pstep, 1)
                pool.wait_ge(s_pstep, 1)
                for m in (ident, ident16):
                    g.affine_select(out=m[:, :], in_=m[:, :], compare_op=ALU.not_equal, fill=1.0,
                                    base=0, pattern=[[-1, N]], channel_multiplier=1)
                g.affine_select(out=rankw[:, :], in_=rankw[:, :], compare_op=ALU.is_ge, fill=0.0,
                                base=0, pattern=[[1, N]], channel_multiplier=-1).then_inc(s_pstep, 1)
                pool.wait_ge(s_pstep, 2)
                g.affine_select(out=rankw[:, :], in_=rankw[:, :], compare_op=ALU.not_equal, fill=KEY,
                                base=0, pattern=[[-1, N]], channel_multiplier=1)
                g.memset(ones16[:, :], 1.0)
                g.memset(ones[:, :], 1.0)
                g.memset(eps_col[:, :], EPS)
                g.memset(hn[:, :, 0:F], 0.0)
                g.iota(key_i[:, :], pattern=[[SC, N // SC + 1]], base=int(KEY), channel_multiplier=0)\
                 .then_inc(s_const, 1)
                pool.wait_ge(s_wmax, 1)
                g.partition_all_reduce(wmax_all[:, :], wmax[:, :], N, bass.bass_isa.ReduceOp.max)\
                 .then_inc(s_wall, 1)

            @block.scalar
            def _(act):
                for dst, src in loads:
                    act.dma_start(dst, src).then_inc(s_w, 16)
                act.wait_ge(s_const, 1)
                layernorm_std(act, 1)

            @block.tensor
            def _(pe):
                pe.wait_ge(s_const, 1)
                pe.wait_ge(s_w, ALL_W)
                nc.tensor.transpose(bank[0][:, 0:N], nm_in[:, :], ident[:, :]).then_inc(s_nmT, 1)
                pe.wait_ge(s_nm, 1)
                nc.tensor.matmul(bank[1][:, 0:B], ones[:, :], nm[:, :], start=True, stop=True).then_inc(s_cnt, 1)

            @block.vector
            def _(dve):
                v = nc.vector
                steps = [0]

                def settled(ins):
                    steps[0] += 1
                    ins.then_inc(s_vstep, 1)
                    dve.wait_ge(s_vstep, steps[0])

                v.memset(wmax[:, :], 0.0)
                v.memset(hT0[F:F + 1, :, :], 1.0)
                v.memset(wac[F:F + 1, H:2 * H], 0.0)
                dve.wait_ge(s_w, ALL_W)
                settled(v.tensor_tensor(wac[0:F, 0:H], w1a[:, :], w1b[:, :], ALU.add))
                v.tensor_copy(wac[0:F, H:2 * H], w1b[:, :])
                settled(v.tensor_scalar(wac[:, 0:H], wac[:, 0:H], -1.0, None, ALU.mult))
                v.tensor_reduce(wmax[0:F + 1, :], wac[:, :], AX.X, ALU.max, apply_absolute_value=True)\
                 .then_inc(s_wmax, 1)
                dve.wait_ge(s_nmT, 1)
                v.tensor_copy(nm[:, :], bank[0][:, 0:B]).then_inc(s_nm, 1)
                dve.wait_ge(s_cnt, 1)
                settled(v.tensor_reduce(cnt_col[:, :], bank[1][:, 0:B], AX.X, ALU.add))
                v.reciprocal(rcnt[:, :], cnt_col[:, :])
                dve.wait_ge(s_wall, 1)
                settled(v.tensor_scalar(wmax_all[:, :], wmax_all[:, :], 2.0 ** -60, None, ALU.max))
                settled(v.tensor_scalar(wexp[:, :].bitcast(I32), wmax_all[:, :].bitcast(I32), 0x7F800000, None,
                                        ALU.bitwise_and))
                v.tensor_scalar(unscale[:, :], wexp[:, :], -(2.0 ** -8), None, ALU.mult)
                settled(v.reciprocal(wscale[:, :], wexp[:, :]))
                settled(v.tensor_scalar(wscale[:, :], wscale[:, :], 2.0 ** 8, None, ALU.mult))
                settled(v.tensor_scalar(wac[:, :], wac[:, :], wscale[0:F + 1, :], None, ALU.mult))
                dve.wait_ge(s_const, 1)
                v.tensor_copy(slot_key[:, :], key_i[:, :])
                for n in range(4):
                    dve.wait_ge(s_x[n], 16)
                    with dve.Fori(0, 4) as j:
                        for e in range(8):
                            last = stats(32 * n + 8 * j + e)
                        last.then_inc(s_bn, 1)
                dve.wait_ge(s_bn, 16)
                layernorm_scales(dve, 1)

        s_adjTp = sem("adj_transposed")
        s_sg = sem("sign_made")
        s_mask = sem("mask_made")
        s_rank = sem("ranks_made")
        s_rs = sem("ranks_copied")
        s_deg = sem("degree_row_copied")
        s_nop = sem("slot_count_step")
        s_n = sem("slot_counts_ready")
        s_np = sem("padding_counted")
        s_npad = sem("padding_copied")
        s_h = sem("h_normalised")
        s_hTp = sem("h_transposed")
        s_hT = sem("h_transpose_copied")
        s_AC = sem("AC_product_made")
        s_hi = sem("AC_high_part_made")
        s_lo = sem("AC_low_part_made")
        s_acc0 = sem("sum_initialised")
        s_G = sem("onehot_chunk_made")
        s_dA = sem("edges_in_bank0")
        s_dB = sem("edges_in_bank1")
        s_fA = sem("bank0_summed")
        s_fB = sem("bank1_summed")
        s_hm = sem("neighbour_sum_ready")
        s_T = sem("sum_transposed")
        s_hmT = sem("sum_transpose_copied")
        s_W2 = sem("layer0_update_made")
        s_x0 = sem("x_updated_layer0")
        s_bn0 = sem("layer1_stats_made")

        pT, pU = bank[6][:, 0:2 * N], bank[7][:, 0:F]
        pA3, pDeg, pH, pAC, pPad = bank[3], bank[4], bank[5], bank[2], bank[4]

        def known(v):
            return isinstance(v, int)

        def pe_adj(pe, g, p, use):
            pe.wait_ge(s_adj[p], use * 16 + 16)
            pe.wait_ge(s_rs, g)
            for q in range(GS):
                last = nc.tensor.transpose(pA3[:, q * N:(q + 1) * N], adj_in[:, p, q * N:(q + 1) * N], ident[:, :])
            last.then_inc(s_adjTp, 1)

        def pe_rank(pe, g, p):
            pe.wait_ge(s_mask, g + 1)
            pe.wait_ge(s_npad, g)
            pe.wait_ge(s_h, g + 1)
            pe.wait_ge(s_hT, g)
            nc.tensor.matmul(pA3[:, :], rankw[:, :], mask[:, p, :], start=True, stop=True)
            nc.tensor.matmul(pDeg[0:1, :], ones16[:, 0:1], mask[:, p, :], start=True, stop=True)
            nc.tensor.matmul(pDeg[F:F + 1, :], ones16[:, 0:1], mask[:, p, :], start=True, stop=True)\
              .then_inc(s_rank, 1)
            for q in range(GS):
                last = nc.tensor.transpose(pH[0:F, q * N:(q + 1) * N], h0[:, q * F:(q + 1) * F], ident[:, :])
            last.then_inc(s_hTp, 1)

        def pe_pad(pe, g, p):
            pe.wait_ge(s_n, g + 1)
            pe.wait_ge(s_deg, g + 1)
            nc.tensor.matmul(pPad[:, 0:GS], ones16[0:1, :], neg_slots[0:1, :], start=True, stop=False)
            for q in range(GS):
                last = nc.tensor.matmul(pPad[:, q:q + 1], mask[:, p, q * N:(q + 1) * N], ones16[:, 0:1],
                                        start=False, stop=(q == GS - 1))
            last.then_inc(s_np, 1)

        def pe_ac(pe, b, g, p, q):
            pe.wait_ge(s_hT, g + 1)
            pe.wait_ge(s_hi, b)
            nc.tensor.matmul(pAC[:, 0:2 * H], hT0[:, p, q * N:(q + 1) * N], wac[:, :], start=True, stop=True)\
              .then_inc(s_AC, 1)

        def pe_transpose_sum(pe, b, par):
            pe.wait_ge(s_hm, b + 1)
            pe.wait_ge(s_hmT, b)
            nc.tensor.transpose(pT[:, 0:N], hm[:, par, 0:N], ident[:, :])
            nc.tensor.transpose(pT[0:H - N, N:2 * N], hm[:, par, N:H], ident[:, :]).then_inc(s_T, 1)

        def pe_update(pe, b, g, p, q):
            pe.wait_ge(s_hmT, b + 1)
            pe.wait_ge(s_deg, g + 1)
            pe.wait_ge(s_x0, b)
            nc.tensor.matmul(pU, hmTa[:, q % 2, :], w2a[:, :], start=True, stop=False)
            nc.tensor.matmul(pU, hmTb[:, p, q * N:(q + 1) * N], w2b[:, :], start=False, stop=True).then_inc(s_W2, 1)

        def pe_slots(pe, b, g, q, cnt, prev):
            pe.wait_ge(s_lo, b + 1)
            pe.wait_ge(s_n, g + 1)
            n = pe.value_load(chunks[0:1, ds(b, 1)], min_val=2, max_val=N // SC)
            with pe.Fori(0, n) as c:
                pe.reg_mov(prev, cnt)
                pe.reg_add(cnt, cnt, 1)
                for half, (ps, free, done) in enumerate(((bank[0], s_fA, s_dA), (bank[1], s_fB, s_dB))):
                    pe.wait_ge(free, prev)
                    for k, part in enumerate((ac_hi, ac_lo)):
                        nc.tensor.matmul(ps[:, 0:2 * H].rearrange("p (t h) -> p t h", t=2), ident16[:, :],
                                         part[:, q, 0:H].unsqueeze(1).broadcast_to([N, 2, H]),
                                         start=(k == 0), stop=False)
                    if half == 0:
                        pe.wait_ge(s_G, cnt)
                    for t in range(2):
                        hot = onehot[:, ds(c * (SC * N) + (2 * half + t) * N, N)]
                        for k, part in enumerate((ac_hi, ac_lo)):
                            last = nc.tensor.matmul(ps[:, t * H:(t + 1) * H], hot, part[:, q, H:2 * H],
                                                    start=False, stop=(k == 1 and t == 1))
                    last.then_inc(done, 1)

        def around(i, body, *more):
            for u in range(2):
                g = 2 * i + u
                for q in range(GS):
                    nxt = None if known(g) and g == NG - 1 else g + 1
                    body(8 * i + 4 * u + q, g, u, q, nxt, 1 - u, i if u == 0 else i + 1)

        def all_iterations(eng, body):
            around(0, body)
            with eng.Fori(1, NI - 1) as i:
                around(i, body)
            around(NI - 1, body)

        def group_of(b, g, u, q, back):
            r = q - back
            if 0 <= r < GS:
                return g, u, r
            return (g - 1, 1 - u, r + GS) if r < 0 else (g + 1, 1 - u, r - GS)

        def act_adj(act, g, p):
            act.wait_ge(s_adjTp, g + 1)
            nc.scalar.activation(adjT[:, ds(g * (GS * N), GS * N)], pA3[:, :], ACT.Copy)
            nc.scalar.activation(sgn[:, :], pA3[:, :], ACT.Sign).then_inc(s_sg, 1)
            act.wait_ge(s_sg, g + 1)
            nc.scalar.activation(mask[:, p, :], sgn[:, :], ACT.Relu).then_inc(s_mask, 1)
            act.wait_ge(s_hTp, g)
            for q in range(GS):
                last = nc.scalar.activation(h0[:, q * F:(q + 1) * F], x[:, ds((g * GS + q) * F, F)], ACT.Relu,
                                            bias=nmr[:, ds(g * GS + q, 1)], scale=rstd[:, ds(g * GS + q, 1)])
            last.then_inc(s_h, 1)

        def act_rank(act, g, p):
            act.wait_ge(s_rank, g + 1)
            for t in range(SC):
                last = nc.scalar.activation(rs[:, p, :, t, :], pA3[:, :].rearrange("p (q j) -> p q j", q=GS),
                                            ACT.Copy, bias=-float(t))
            last.then_inc(s_rs, 1)
            act.wait_ge(s_hTp, g + 1)
            nc.scalar.activation(hT0[0:F, p, :], pH[0:F, :], ACT.Copy).then_inc(s_hT, 1)

        def act_pad(act, g, p):
            act.wait_ge(s_np, g + 1)
            nc.scalar.activation(neg_pad[:, p, :], pPad[:, 0:GS], ACT.Copy, scale=0.5).then_inc(s_npad, 1)

        def act_degrees(act, g, p, updates):
            act.wait_ge(s_rank, g + 1)
            if updates is not None:
                act.wait_ge(s_W2, updates)
            nc.scalar.activation(hmTb[F:F + 1, p, :], pDeg[F:F + 1, :], ACT.Copy).then_inc(s_deg, 1)

        def act_ac(act, b, q):
            act.wait_ge(s_AC, b + 1)
            if not (known(b) and b < 2):
                act.wait_ge(s_lo, b - 1)
                act.wait_ge(s_acc0, b - 1)
            nc.scalar.activation(ac32[:, q % 2, :], pAC[:, 0:2 * H], ACT.Copy)
            nc.scalar.activation(ac_hi[:, q, :], pAC[:, 0:2 * H], ACT.Copy).then_inc(s_hi, 1)

        def act_init(act, b, g, p, q):
            act.wait_ge(s_npad, g + 1)
            act.wait_ge(s_hi, b + 1)
            if not (known(b) and b < 4):
                act.wait_ge(s_hm, b - 3)
            nc.scalar.activation(acc[:, q, :].rearrange("p (t h) -> p t h", t=2),
                                 ac32[:, q % 2, 0:H].unsqueeze(1).broadcast_to([N, 2, H]), ACT.Relu,
                                 scale=neg_pad[:, p, q:q + 1]).then_inc(s_acc0, 1)

        def act_sum(act, b, p, q):
            act.wait_ge(s_T, b + 1)
            nc.scalar.activation(hmTa[:, q % 2, :], pT[:, 0:N], ACT.Copy, scale=unscale[:, 0:1])
            nc.scalar.activation(hmTb[0:H - N, p, q * N:(q + 1) * N], pT[0:H - N, N:2 * N], ACT.Copy,
                                 scale=unscale[0:H - N, 0:1]).then_inc(s_hmT, 1)

        def dve_counts(dve, g):
            dve.wait_ge(s_rank, g + 1)
            nc.vector.tensor_reduce(maxdeg[:, :], pDeg[0:1, :].rearrange("p (q j) -> p q j", q=GS), AX.X, ALU.max)\
              .then_inc(s_nop, 1)
            dve.wait_ge(s_nop, 3 * g + 1)
            nc.vector.tensor_scalar(maxdeg_i[:, :], maxdeg[:, :], float(SC + 1), float(SC - 1), ALU.max, ALU.add)\
              .then_inc(s_nop, 1)
            dve.wait_ge(s_nop, 3 * g + 2)
            nc.vector.tensor_scalar(chunks[:, ds(g * GS, GS)], maxdeg_i[:, :], 2, None, ALU.arith_shift_right)\
              .then_inc(s_nop, 1)
            dve.wait_ge(s_nop, 3 * g + 3)
            if not (known(g) and g == 0):
                dve.wait_ge(s_np, g)
            nc.vector.tensor_scalar(neg_slots[:, :], chunks[:, ds(g * GS, GS)], -float(SC), None, ALU.mult)\
              .then_inc(s_n, 1)

        def dve_onehot(p, q, c):
            nc.vector.tensor_scalar(onehot[:, ds(c * (SC * N), SC * N)],
                                    rs[:, p, q, :, :].rearrange("p t j -> p (t j)"),
                                    slot_key[:, ds(c, 1)], None, ALU.is_equal).then_inc(s_G, 1)

        def dve_slots(dve, b, g, u, q, cnt, prev):
            dve.wait_ge(s_acc0, b + 1)
            dve.wait_ge(s_n, g + 1)
            n = dve.value_load(chunks[0:1, ds(b, 1)], min_val=2, max_val=N // SC)

            def chunk():
                a2 = acc[:, q, :]
                dve.wait_ge(s_dA, cnt)
                dve.wait_ge(s_fB, prev)
                nc.vector.scalar_tensor_tensor(out=a2, in0=bank[0][:, 0:2 * H], scalar=0.0, in1=a2,
                                               op0=ALU.min, op1=ALU.add).then_inc(s_fA, 1)
                dve.wait_ge(s_dB, cnt)
                dve.wait_ge(s_fA, cnt)
                nc.vector.scalar_tensor_tensor(out=a2, in0=bank[1][:, 0:2 * H], scalar=0.0, in1=a2,
                                               op0=ALU.min, op1=ALU.add).then_inc(s_fB, 1)

            with dve.Fori(0, n - 1) as c:
                dve.reg_mov(prev, cnt)
                dve.reg_add(cnt, cnt, 1)
                dve_onehot(u, q, c + 1)
                chunk()
            dve.reg_mov(prev, cnt)
            dve.reg_add(cnt, cnt, 1)
            if not (known(b) and b == B - 1):
                g1, p1, q1 = group_of(b, g, u, q, -1)
                dve.wait_ge(s_rs, g1 + 1)
                dve_onehot(p1, q1, 0)
            chunk()

        def dve_update(dve, b):
            xb = x[:, ds(b * F, F)]
            dve.wait_ge(s_x0, b)
            dve.wait_ge(s_W2, b + 1)
            nc.vector.tensor_tensor(xb, pU, xb, ALU.add).then_inc(s_x0, 1)
            if not (known(b) and b == 0):
                stats(b - 1)

        def pool_low(pool, b, q):
            pool.wait_ge(s_hi, b + 1)
            nc.gpsimd.tensor_tensor(ac_lo[:, q, :], ac32[:, q % 2, :], ac_hi[:, q, :], ALU.subtract)\
              .then_inc(s_lo, 1)

        def pool_sum(pool, b, g, q, total):
            pool.wait_ge(s_n, g + 1)
            n = pool.value_load(chunks[0:1, ds(b, 1)], min_val=2, max_val=N // SC)
            pool.reg_add(total, total, n)
            pool.wait_ge(s_fB, total)
            nc.gpsimd.tensor_tensor(hm[:, q % 2, :], acc[:, q, 0:H], acc[:, q, H:2 * H], ALU.add).then_inc(s_hm, 1)

        with nc.Block() as block:
            @block.sync
            def _(sp):
                with sp.Fori(1, NI) as i:
                    for p in range(2):
                        sp.wait_ge(s_adjTp, 2 * i + p - 1)
                        load_adj(sp, 2 * i + p, p)

            @block.tensor
            def _(pe):
                cnt, prev = pe.alloc_register("pe_chunk"), pe.alloc_register("pe_chunk_before")
                pe.reg_mov(cnt, 0)
                pe_adj(pe, 0, 0, 0)
                pe_rank(pe, 0, 0)
                pe_pad(pe, 0, 0)
                pe_ac(pe, 0, 0, 0, 0)
                pe_ac(pe, 1, 0, 0, 1)

                def step(b, g, u, q, nxt, p, use):
                    if nxt is not None:
                        if q == 0:
                            pe_adj(pe, nxt, p, use)
                        if q == 1:
                            pe_rank(pe, nxt, p)
                        if q == 3:
                            pe_pad(pe, nxt, p)
                    if not (known(b) and b + 2 >= B):
                        pe_ac(pe, b + 2, *group_of(b, g, u, q, -2))
                    if not (known(b) and b < 2):
                        pe_transpose_sum(pe, b - 2, q % 2)
                    if not (known(b) and b < 3):
                        pe_update(pe, b - 3, *group_of(b, g, u, q, 3))
                    pe_slots(pe, b, g, q, cnt, prev)

                all_iterations(pe, step)
                pe_transpose_sum(pe, B - 2, 0)
                pe_update(pe, B - 3, NG - 1, 1, 1)
                pe_transpose_sum(pe, B - 1, 1)
                pe_update(pe, B - 2, NG - 1, 1, 2)
                pe_update(pe, B - 1, NG - 1, 1, 3)

            @block.scalar
            def _(act):
                act_adj(act, 0, 0)
                act_rank(act, 0, 0)
                act_degrees(act, 0, 0, None)
                act_pad(act, 0, 0)
                act_ac(act, 0, 0)
                act_ac(act, 1, 1)
                act_init(act, 0, 0, 0, 0)

                def step(b, g, u, q, nxt, p, use):
                    if nxt is not None:
                        if q == 0:
                            act_adj(act, nxt, p)
                        if q == 1:
                            act_rank(act, nxt, p)
                        if q == 3:
                            act_degrees(act, nxt, p, None if known(nxt) and nxt < 2 else GS * nxt - GS)
                    if not (known(b) and b + 2 >= B):
                        act_ac(act, b + 2, (q + 2) % GS)
                    if not (known(b) and b < 2):
                        act_sum(act, b - 2, *group_of(b, g, u, q, 2)[1:])
                    if nxt is not None and q == 3:
                        act_pad(act, nxt, p)
                    if not (known(b) and b + 1 >= B):
                        act_init(act, b + 1, *group_of(b, g, u, q, -1))

                all_iterations(act, step)
                act_sum(act, B - 2, 1, 2)
                act_sum(act, B - 1, 1, 3)

            @block.vector
            def _(dve):
                cnt, prev = dve.alloc_register("dve_chunk"), dve.alloc_register("dve_chunk_before")
                dve.reg_mov(cnt, 0)
                dve_counts(dve, 0)
                dve.wait_ge(s_rs, 1)
                dve_onehot(0, 0, 0)

                def step(b, g, u, q, nxt, p, use):
                    if nxt is not None and q == 2:
                        dve_counts(dve, nxt)
                    dve_slots(dve, b, g, u, q, cnt, prev)
                    if not (known(b) and b < 3):
                        dve_update(dve, b - 3)

                all_iterations(dve, step)
                for b in range(B - 3, B):
                    dve_update(dve, b)
                dve.wait_ge(s_x0, B)
                stats(B - 1).then_inc(s_bn0, 1)

            @block.gpsimd
            def _(pool):
                total = pool.alloc_register("pool_chunks")
                pool.reg_mov(total, 0)
                pool_low(pool, 0, 0)
                pool_low(pool, 1, 1)

                def step(b, g, u, q, nxt, p, use):
                    if not (known(b) and b + 2 >= B):
                        pool_low(pool, b + 2, (q + 2) % GS)
                    pool_sum(pool, b, g, q, total)

                all_iterations(pool, step)

        s_hn1 = [sem(f"l1_h_normalised{u}") for u in range(2)]
        s_p1 = [sem(f"l1_stage_done{u}") for u in range(2)]
        s_c1 = [sem(f"l1_stage_copied{u}") for u in range(2)]
        s_t1 = [sem(f"l1_update_step{u}") for u in range(2)]
        s_bn1 = sem("layer2_stats_made")
        ST = 8

        def norm_graph(s_done, u, b, q, last):
            ins = nc.scalar.activation(hn[:, u, (q + 1) * F:(q + 2) * F], x[:, ds((b + q) * F, F)], ACT.Relu,
                                       bias=nmr[:, ds(b + q, 1)], scale=rstd[:, ds(b + q, 1)])
            if last:
                ins.then_inc(s_done, 1)

        def grp(u, i):
            return 2 * i + u

        with nc.Block() as block:
            @block.tensor
            def _(pe):
                turn = [pe.alloc_register(f"l1_turn{u}") for u in range(2)]
                for u in range(2):
                    pe.reg_mov(turn[u], 1)
                with pe.Fori(0, NI) as i:
                    for st in range(ST):
                        for u in range(2):
                            ps = bank[4 * u + (st % 2)]
                            b0 = GS * grp(u, i)
                            pe.wait_ge(s_c1[u], ST * i + st)
                            if st == 0:
                                pe.wait_ge(s_hn1[u], turn[u])
                                pe.reg_add(turn[u], turn[u], 1)
                            for q in range(GS):
                                cols = slice(q * N, (q + 1) * N)
                                if st == 0:
                                    last = nc.tensor.transpose(ps[0:F, cols], hn[:, u, (q + 1) * F:(q + 2) * F], ident[:, :])
                                elif st == 1:
                                    last = nc.tensor.matmul(ps[:, cols], hT[:, u, cols], l1w0[:, :], start=True, stop=True)
                                elif st in (2, 4, 6):
                                    last = nc.tensor.matmul(ps[:, cols], msg[:, u, cols],
                                                            adjT[:, ds((b0 + q) * N, N)], start=True, stop=True)
                                elif st in (3, 5):
                                    w = l1w1 if st == 3 else l1w2
                                    last = nc.tensor.matmul(ps[:, cols], hid[:, u, cols], w[:, :], start=True, stop=True)
                                else:
                                    last = nc.tensor.matmul(ps[:, q * F:(q + 1) * F], hid[:, u, cols], l1wo[:, :],
                                                            start=True, stop=True)
                            last.then_inc(s_p1[u], 1)

            @block.scalar
            def _(act):
                layernorm_std(act, 2)
                act.wait_ge(s_ln, 2)
                for u in range(2):
                    for q in range(GS):
                        norm_graph(s_hn1[u], u, GS * u, q, q == GS - 1)

                def group_pair(i, more):
                    for st in range(ST):
                        for u in range(2):
                            if st in (0, 2, 4, 6):
                                act.wait_ge(s_p1[u], ST * i + st + 1)
                            ps = bank[4 * u + (st % 2)]
                            if st == 0:
                                nc.scalar.activation(hT[0:F, u, :], ps[0:F, :], ACT.Copy).then_inc(s_c1[u], 1)
                            elif st in (2, 4, 6):
                                nc.scalar.activation(hid[:, u, :], ps[:, :], ACT.Relu).then_inc(s_c1[u], 1)
                            elif more:
                                q = st // 2
                                norm_graph(s_hn1[u], u, GS * grp(u, i + 1), q, q == GS - 1)

                with act.Fori(0, NI - 1) as i:
                    group_pair(i, True)
                group_pair(NI - 1, False)

            @block.vector
            def _(dve):
                dve.wait_ge(s_bn0, 1)
                layernorm_scales(dve, 2)

                def group_pair(i):
                    for st in (1, 3, 5):
                        for u in range(2):
                            ps = bank[4 * u + (st % 2)]
                            dve.wait_ge(s_p1[u], ST * i + st + 1)
                            if st == 1:
                                nc.vector.tensor_copy(msg[:, u, :], ps[:, :]).then_inc(s_c1[u], 1)
                            else:
                                bias = l1b1 if st == 3 else l1b2
                                nc.vector.tensor_tensor(
                                    msg[:, u, :].rearrange("p (q d) -> p q d", q=GS),
                                    ps[:, :].rearrange("p (q d) -> p q d", q=GS),
                                    bias[:, :].unsqueeze(1).broadcast_to([N, GS, D1]), ALU.add).then_inc(s_c1[u], 1)
                    for u in range(2):
                        ps = bank[4 * u + 1]
                        b0 = GS * grp(u, i)
                        up3 = upd[:, u, :].rearrange("p (q f) -> p q f", q=GS)
                        xg = x[:, ds(b0 * F, GS * F)]
                        dve.wait_ge(s_p1[u], ST * i + ST)
                        nc.vector.tensor_tensor(up3, ps[:, 0:GS * F].rearrange("p (q f) -> p q f", q=GS),
                                                l1bo[:, :].unsqueeze(1).broadcast_to([N, GS, F]), ALU.add)\
                          .then_inc(s_c1[u], 1)
                        dve.wait_ge(s_c1[u], ST * i + ST)
                        nc.vector.tensor_tensor(up3, up3, nm[:, ds(b0, GS)].unsqueeze(2).broadcast_to([N, GS, F]),
                                                ALU.mult).then_inc(s_t1[u], 1)
                        dve.wait_ge(s_t1[u], 2 * i + 1)
                        nc.vector.tensor_tensor(xg, xg, upd[:, u, :], ALU.add).then_inc(s_t1[u], 1)

                def pair_stats(i):
                    for e in range(2 * GS):
                        last = stats(2 * GS * i + e)
                    return last

                with dve.Fori(0, NI) as i:
                    group_pair(i)
                    for u in range(2):
                        dve.wait_ge(s_t1[u], 2 * i + 2)
                    pair_stats(i).then_inc(s_bn1, 1)

        s_hn2 = [sem(f"l2_h_normalised{u}") for u in range(2)]
        s_p2 = [sem(f"l2_stage_done{u}") for u in range(2)]
        s_c2 = [sem(f"l2_stage_copied{u}") for u in range(2)]
        s_q2 = [sem(f"l2_squares_made{u}") for u in range(2)]
        s_n2 = [sem(f"l2_row_sums_made{u}") for u in range(2)]

        with nc.Block() as block:
            @block.tensor
            def _(pe):
                with pe.Fori(0, NI) as i:
                    for st in range(2):
                        for u in range(2):
                            ps = bank[4 * u + st]
                            b0 = GS * grp(u, i)
                            pe.wait_ge(s_c2[u], 2 * i + st)
                            if st == 0:
                                pe.wait_ge(s_hn2[u], i + 1)
                            for q in range(GS):
                                cols = slice(q * N, (q + 1) * N)
                                if st == 0:
                                    hq = hn[:, u, (q + 1) * F:(q + 2) * F]
                                    nc.tensor.matmul(ps[0:F, cols], hq, adjT[:, ds((b0 + q) * N, N)],
                                                     start=True, stop=False)
                                    last = nc.tensor.matmul(ps[0:F, cols], hq, ident[:, :], start=False, stop=True)
                                else:
                                    last = nc.tensor.matmul(ps[:, q * F:(q + 1) * F], hT[:, u, cols], l2w[:, :],
                                                            start=True, stop=True)
                            last.then_inc(s_p2[u], 1)

            @block.scalar
            def _(act):
                layernorm_std(act, 3)
                act.wait_ge(s_ln, 3)
                for u in range(2):
                    for q in range(GS):
                        norm_graph(s_hn2[u], u, GS * u, q, q == GS - 1)

                def group_pair(i, more):
                    if more:
                        for u in range(2):
                            act.wait_ge(s_p2[u], 2 * i + 1)
                            for q in range(GS):
                                norm_graph(s_hn2[u], u, GS * grp(u, i + 1), q, q == GS - 1)
                    for u in range(2):
                        b0 = GS * grp(u, i)
                        act.wait_ge(s_p2[u], 2 * i + 2)
                        nc.scalar.activation(y[:, ds(b0 * F, GS * F)], bank[4 * u + 1][:, 0:GS * F], ACT.Copy)
                        act.wait_ge(s_n2[u], i)
                        nc.scalar.activation(upd[:, u, :], bank[4 * u + 1][:, 0:GS * F], ACT.Square)\
                          .then_inc(s_c2[u], 1)

                with act.Fori(0, NI - 1) as i:
                    group_pair(i, True)
                group_pair(NI - 1, False)

            @block.vector
            def _(dve):
                dve.wait_ge(s_bn1, NI)
                layernorm_scales(dve, 3)
                with dve.Fori(0, NI) as i:
                    for u in range(2):
                        dve.wait_ge(s_p2[u], 2 * i + 1)
                        nc.vector.tensor_copy(hT[0:F, u, :], bank[4 * u][0:F, :]).then_inc(s_c2[u], 1)
                    for u in range(2):
                        dve.wait_ge(s_c2[u], 2 * i + 2)
                        nc.vector.tensor_reduce(ss[:, ds(GS * grp(u, i), GS)],
                                                upd[:, u, :].rearrange("p (q f) -> p q f", q=GS), AX.X, ALU.add)\
                          .then_inc(s_n2[u], 1)

        s_nrm = sem("row_norms_ready")
        s_y = sem("y_chunk_normalised")
        s_ym = sem("y_chunk_masked")
        s_yms = sem("y_masked_chunk_summed")
        s_vb = sem("batchnorm_step")
        s_mean = sem("batchnorm_mean_ready")
        s_d = sem("y_chunk_centred")
        s_dq = sem("y_chunk_squared")
        s_dm = sem("y_square_masked")
        s_dms = sem("y_square_chunk_summed")
        s_var = sem("batchnorm_std_ready")
        s_ya = sem("y_chunk_scaled")
        s_yb = sem("y_chunk_shifted")
        s_yc = sem("y_chunk_shifted_masked")
        s_xn = sem("x_updated_layer2")
        s_bn2 = sem("layer3_stats_made")

        def yc(c):
            return y[:, ds(c * XC, XC)]

        def g3(ap):
            return ap.rearrange("p (g f) -> p g f", f=F)

        def per_graph(t, c):
            return t[:, ds(c * GX, GX)].unsqueeze(2).broadcast_to([N, GX, F])

        def per_feature(t):
            return t.unsqueeze(1).broadcast_to([N, GX, F])

        with nc.Block() as block:
            @block.tensor
            def _(pe):
                def add(ps, k, src, ready, done, first, last):
                    pe.wait_ge(ready, k + 1)
                    nc.tensor.matmul(ps[:, :], ones[:, :], src, start=first, stop=last).then_inc(done, 1)

                for ps, off, ready, done in ((bank[0], 0, s_ym, s_yms), (bank[1], 2, s_dm, s_dms)):
                    add(ps, 0, tmp[:, off, :], ready, done, True, False)
                    for k in range(1, NXC):
                        add(ps, k, tmp[:, off + k % 2, :], ready, done, False, k == NXC - 1)

            @block.vector
            def _(dve):
                v = nc.vector
                steps = [0]

                def settled(ins):
                    steps[0] += 1
                    ins.then_inc(s_vb, 1)
                    dve.wait_ge(s_vb, steps[0])

                dve.wait_ge(s_nrm, 1)
                settled(v.tensor_scalar(ss[:, :], ss[:, :], 1e-12, None, ALU.max))
                settled(v.reciprocal(ss[:, :], ss[:, :]))
                with dve.Fori(0, NXC) as c:
                    v.tensor_tensor(g3(yc(c)), g3(yc(c)), per_graph(ss, c), ALU.mult).then_inc(s_y, 1)
                dve.wait_ge(s_yms, NXC)
                settled(v.tensor_reduce(stat[:, 0, :], bank[0][:, :].rearrange("p (g f) -> p f g", f=F), AX.X, ALU.add))
                v.tensor_scalar(stat[:, 1, :], stat[:, 0, :], rcnt[:, :], None, ALU.mult).then_inc(s_mean, 1)
                dve.wait_ge(s_mean, 1)
                with dve.Fori(0, NXC) as c:
                    v.tensor_tensor(g3(yc(c)), g3(yc(c)), per_feature(stat[:, 1, :]), ALU.subtract).then_inc(s_d, 1)
                dve.wait_ge(s_dms, NXC)
                settled(v.tensor_reduce(stat[:, 2, :], bank[1][:, :].rearrange("p (g f) -> p f g", f=F), AX.X, ALU.add))
                settled(v.tensor_scalar(stat[:, 3, :], stat[:, 2, :], rcnt[:, :], None, ALU.mult))
                dve.wait_ge(s_var, 1)
                settled(v.reciprocal(stat[:, 5, :], stat[:, 4, :]))
                settled(v.tensor_tensor(stat[:, 5, :], stat[:, 5, :], gamma[:, :], ALU.mult))
                with dve.Fori(0, NXC) as c:
                    v.tensor_tensor(g3(yc(c)), g3(yc(c)), per_feature(stat[:, 5, :]), ALU.mult).then_inc(s_ya, 1)
                with dve.Fori(0, NXC) as c:
                    xc = x[:, ds(c * XC, XC)]
                    dve.wait_ge(s_yc, c + 1)
                    v.scalar_tensor_tensor(out=xc, in0=yc(c), scalar=0.0, in1=xc, op0=ALU.max, op1=ALU.add)\
                     .then_inc(s_xn, 1)
                    dve.wait_ge(s_xn, c + 1)
                    for e in range(GX):
                        last = stats(c * GX + e)
                    last.then_inc(s_bn2, 1)
                dve.wait_ge(s_bn2, NXC)
                layernorm_scales(dve, 4)

            @block.scalar
            def _(act):
                act.activation(ss[:, :], ss[:, :], ACT.Sqrt).then_inc(s_nrm, 1)
                for c in range(NXC):
                    act.wait_ge(s_d, c + 1)
                    if c >= 2:
                        act.wait_ge(s_dms, c - 1)
                    act.activation(tmp[:, 2 + c % 2, :], yc(c), ACT.Square).then_inc(s_dq, 1)
                act.wait_ge(s_vb, 5)
                act.activation(stat[:, 4, :], stat[:, 3, :], ACT.Sqrt, bias=eps_col[:, 0:1]).then_inc(s_var, 1)
                layernorm_std(act, 4)

            @block.gpsimd
            def _(pool):
                g = nc.gpsimd
                for c in range(NXC):
                    pool.wait_ge(s_y, c + 1)
                    if c >= 2:
                        pool.wait_ge(s_yms, c - 1)
                    g.tensor_tensor(g3(tmp[:, c % 2, :]), g3(yc(c)), per_graph(nm, c), ALU.mult).then_inc(s_ym, 1)
                for c in range(NXC):
                    pool.wait_ge(s_dq, c + 1)
                    t = g3(tmp[:, 2 + c % 2, :])
                    g.tensor_tensor(t, t, per_graph(nm, c), ALU.mult).then_inc(s_dm, 1)
                with pool.Fori(0, NXC) as c:
                    pool.wait_ge(s_ya, c + 1)
                    g.tensor_tensor(g3(yc(c)), g3(yc(c)), per_feature(beta[:, :]), ALU.add).then_inc(s_yb, 1)
                    pool.wait_ge(s_yb, c + 1)
                    g.tensor_tensor(g3(yc(c)), g3(yc(c)), per_graph(nm, c), ALU.mult).then_inc(s_yc, 1)

        s_hn3 = [sem(f"l3_h_normalised{u}") for u in range(2)]
        s_p3 = [sem(f"l3_stage_done{u}") for u in range(2)]
        s_c3 = [sem(f"l3_stage_copied{u}") for u in range(2)]
        s_out = [sem(f"stored{u}") for u in range(2)]

        with nc.Block() as block:
            @block.tensor
            def _(pe):
                with pe.Fori(0, NI) as i:
                    for st in range(3):
                        for u in range(2):
                            ps = bank[4 * u + st]
                            b0 = GS * grp(u, i)
                            pe.wait_ge(s_c3[u], 3 * i + st)
                            if st == 0:
                                pe.wait_ge(s_hn3[u], i + 1)
                                for q in range(GS):
                                    cols = slice(q * N, (q + 1) * N)
                                    hq = hn[:, u, (q + 1) * F:(q + 2) * F]
                                    nc.tensor.matmul(ps[:, cols], hn[:, u, q * F:(q + 2) * F],
                                                     adjT[:, ds((b0 + q) * N, N)], start=True, stop=True)
                                    last = nc.tensor.transpose(ps[0:F, cols], hq, ident[:, :])
                            elif st == 1:
                                last = nc.tensor.matmul(ps[0:F, :], l3w1[:, :], msg[:, u, :], start=True, stop=True)
                            else:
                                for q in range(GS):
                                    cols = slice(q * N, (q + 1) * N)
                                    last = nc.tensor.matmul(ps[:, q * F:(q + 1) * F], hT[:, u, cols], l3w2[:, :],
                                                            start=True, stop=True)
                            last.then_inc(s_p3[u], 1)

            @block.scalar
            def _(act):
                nc.scalar.activation(std[:, 0:1], eps_col[:, 0:1], ACT.Tanh)
                act.wait_ge(s_ln, 4)
                for u in range(2):
                    for q in range(GS):
                        norm_graph(s_hn3[u], u, GS * u, q, q == GS - 1)

                def group_pair(i, more):
                    for u in range(2):
                        act.wait_ge(s_p3[u], 3 * i + 2)
                        nc.scalar.activation(hT[0:F, u, :], bank[4 * u + 1][0:F, :], ACT.Tanh, bias=l3b1[:, 0:1])\
                          .then_inc(s_c3[u], 1)
                        if more:
                            for q in range(GS):
                                norm_graph(s_hn3[u], u, GS * grp(u, i + 1), q, q == GS - 1)

                with act.Fori(0, NI - 1) as i:
                    group_pair(i, True)
                group_pair(NI - 1, False)

            @block.vector
            def _(dve):
                with dve.Fori(0, NI) as i:
                    for u in range(2):
                        dve.wait_ge(s_p3[u], 3 * i + 1)
                        nc.vector.tensor_copy(msg[:, u, :], bank[4 * u][:, :]).then_inc(s_c3[u], 1)
                    for u in range(2):
                        dve.wait_ge(s_p3[u], 3 * i + 3)
                        dve.wait_ge(s_out[u], 16 * i)
                        nc.vector.tensor_tensor(upd[:, u, :], bank[4 * u + 2][:, 0:GS * F],
                                                x[:, ds(GS * grp(u, i) * F, GS * F)], ALU.add).then_inc(s_c3[u], 1)

            @block.sync
            def _(sp):
                with sp.Fori(0, NI) as i:
                    for u in range(2):
                        sp.wait_ge(s_c3[u], 3 * i + 3)
                        sp.dma_start(out_v[:, ds(GS * grp(u, i), GS), :],
                                     upd[:, u, :].rearrange("p (q f) -> p q f", q=GS)).then_inc(s_out[u], 16)
                for u in range(2):
                    sp.wait_ge(s_out[u], 16 * NI)


_INS = ["x", "adj", "nodemask", "L0_gnn_W1", "L0_gnn_b1", "L0_gnn_W2", "L0_gnn_b2",
        "L1_gnn_W0", "L1_gnn_b0", "L1_gnn_W1", "L1_gnn_b1", "L1_gnn_W2", "L1_gnn_b2",
        "L1_gnn_Wout", "L1_gnn_bout", "L2_gnn_weight", "L2_gnn_bias", "L2_gnn_gamma",
        "L2_gnn_beta", "L3_gnn_W1", "L3_gnn_b1", "L3_gnn_W2", "L3_gnn_b2"]
_OUTS = [((128, 128, 64), "float32")]


def kernel(**inputs):
    import numpy as _np
    import concourse.bacc as _bacc
    from concourse import mybir as _mybir
    from concourse.bass_utils import run_bass_kernel_spmd as _run

    nc = _bacc.Bacc("TRN2", target_bir_lowering=False, num_devices=1)
    arrays, args = {}, {}
    for name in _INS:
        v = _np.ascontiguousarray(inputs[name])
        arrays[f"in_{name}_dram"] = v
        args[name] = nc.dram_tensor(f"in_{name}_dram", v.shape, _mybir.dt.from_np(v.dtype), kind="ExternalInput").ap()
    outs = [nc.dram_tensor(f"out_{i}_dram", s, _mybir.dt.from_np(_np.dtype(d)), kind="ExternalOutput").ap()
            for i, (s, d) in enumerate(_OUTS)]
    gnn_stack_kernel(nc, args, outs[0])
    r = _run(nc, [arrays], core_ids=[0])
    return r.results[0]["out_0_dram"]
```

```python
import concourse.bass as bass
from concourse import mybir
from contextlib import ExitStack

F32 = mybir.dt.float32
F16 = mybir.dt.float16
I32 = mybir.dt.int32
ALU = mybir.AluOpType
ACT = mybir.ActivationFunctionType
AX = mybir.AxisListType


def gnn_stack_kernel(nc, a, out):
    B, N, F = a["x"].shape
    H = a["L0_gnn_W2"].shape[0]
    D1 = a["L1_gnn_W0"].shape[1]
    GS = 4
    NG = B // GS
    NI = NG // 2
    BANKS = [(0, 0, 2), (1, 2, 2), (5, 4, 2), (6, 6, 1)]
    SC = 7
    MAXC = -(-N // SC)
    DIV, SH = 9363, 16
    EPS = 1e-5
    KEY = 257.0
    XC = 512
    NXC = B * F // XC
    GX = XC // F

    ctx = ExitStack()
    with ctx:
        def sb(name, shape, dt=F32):
            return ctx.enter_context(nc.sbuf_tensor(name, shape, dt))

        def sem(name):
            return ctx.enter_context(nc.semaphore(name))

        x = sb("x_all", [N, B * F])
        adjT = sb("adjT_all", [N, B * N])
        ident = sb("ident", [N, N])
        ident16 = sb("ident16", [N, N], F16)
        rankw = sb("rankw", [N, N], F16)
        ones16 = sb("ones16", [N, N], F16)
        ones = sb("ones", [N, N])
        key_i = sb("key_i", [N, MAXC + 1], I32)
        slot_key = sb("slot_key", [N, MAXC + 1])
        eps_col = sb("eps_col", [N, 1])
        w1a = sb("w1a", [F, H])
        w1b = sb("w1b", [F, H])
        wac = sb("wac", [F + 1, 2 * H])
        wmax = sb("wmax", [N, 1])
        wmax_all = sb("wmax_all", [N, 1])
        wexp = sb("wexp", [N, 1])
        wscale = sb("wscale", [N, 1])
        unscale = sb("unscale", [N, 1])
        w2a = sb("w2a", [N, F])
        w2b = sb("w2b", [H - N + 1, F])
        l1w0 = sb("l1w0", [F + 1, D1])
        l1w1 = sb("l1w1", [D1, D1])
        l1w2 = sb("l1w2", [D1, D1])
        l1wo = sb("l1wo", [D1, F])
        l1b1 = sb("l1b1", [N, D1])
        l1b2 = sb("l1b2", [N, D1])
        l1bo = sb("l1bo", [N, F])
        l2w = sb("l2w", [F + 1, F])
        gamma = sb("gamma", [N, F])
        beta = sb("beta", [N, F])
        l3w1 = sb("l3w1", [2 * F, F])
        l3b1 = sb("l3b1", [F, 1])
        l3w2 = sb("l3w2", [F + 1, F])
        nm_in = sb("nm_in", [B, N])
        nm = sb("nm", [N, B])
        rcnt = sb("rcnt", [N, 1])
        cnt_col = sb("cnt_col", [N, 1])
        bn6 = sb("bn6", [N, B, 6])
        var = sb("var", [N, B])
        dif = sb("dif", [N, B])
        msum = sb("msum", [N, B])
        std = sb("std", [N, B])
        rstd = sb("rstd", [N, B])
        nmr = sb("nmr", [N, B])
        adj_in = sb("adj_in", [N, 2, GS * N])
        sgn = sb("sgn", [N, GS * N], F16)
        mask = sb("mask", [N, 2, GS * N], F16)
        rs = sb("rs", [N, 2, GS, SC, N], F16)
        onehot = sb("onehot", [N, MAXC * SC * N], F16)
        y = onehot[:, 0:2 * B * F].bitcast(F32)
        maxdeg = sb("maxdeg", [1, GS])
        maxdeg_i = sb("maxdeg_i", [1, GS], I32)
        chunks = sb("chunks", [1, B], I32)
        neg_slots = sb("neg_slots", [1, GS], F16)
        neg_pad = sb("neg_pad", [N, 2, GS])
        h0 = sb("h0", [N, GS * F])
        hT0 = sb("hT0", [F + 1, 2, GS * N])
        ac32 = sb("ac32", [N, 2, 2 * H])
        ac_hi = sb("ac_hi", [N, 4, 2 * H], F16)
        ac_lo = sb("ac_lo", [N, 4, 2 * H], F16)
        acc = sb("acc", [N, 4, 4 * H])
        hm = sb("hm", [N, 2, H])
        hmTa = sb("hmTa", [N, 2, N])
        hmTb = sb("hmTb", [H - N + 1, 2, GS * N])
        hn = sb("hn", [N, 2, (GS + 1) * F])
        hT = hT0
        msg = adj_in
        hid = acc[:, 0:2, 0:GS * N]
        upd = acc[:, 2:4, 0:GS * F]
        ss = sb("ss", [N, B])
        tmp = rs[:, :, :, :, :].rearrange("p u q t j -> p (u q t j)")[:, 0:8 * XC].bitcast(F32)\
            .rearrange("p (a c) -> p a c", c=XC)
        stat = sb("stat", [N, 6, F])

        bank = [ctx.enter_context(nc.psum_tensor(f"bank{n}", [N, 512], F32)) for n in range(8)]

        adj_v = a["adj"].rearrange("b i j -> i b j")
        x_v = a["x"].rearrange("b n f -> n b f")
        out_v = out.rearrange("b n f -> n b f")
        x3 = x[:, :].rearrange("p (b f) -> p b f", f=F)
        ds = bass.ds

        s_w0 = sem("layer0_weights_loaded")
        s_w = sem("later_weights_loaded")
        s_x = [sem(f"x_loaded{n}") for n in range(4)]
        s_adj = [sem(f"adj_loaded{p}") for p in range(2)]
        s_const = sem("constants_made")
        s_pstep = sem("pool_setup_step")
        s_vstep = sem("vector_setup_step")
        s_wmax = sem("weight_max_ready")
        s_wall = sem("weight_max_spread")
        s_nmT = sem("nodemask_transposed")
        s_nm = sem("nodemask_copied")
        s_cnt = sem("nodemask_counted")
        s_bn = sem("layernorm_stats_made")
        s_lnstep = sem("layernorm_step")
        s_var64 = sem("variances_ready")
        s_std = sem("std_ready")
        s_rstd = sem("rstd_ready")
        s_ln = sem("layernorm_scales_ready")

        def row(ap, n):
            return ap.rearrange("(a n) -> a n", a=1)

        def spread(ap, n):
            return ap.unsqueeze(0).broadcast_to([N, n])

        loads0 = [
            (w1a[:, :], a["L0_gnn_W1"][0:F, :]), (w1b[:, :], a["L0_gnn_W1"][F:2 * F, :]),
            (wac[F:F + 1, 0:H], row(a["L0_gnn_b1"], H)),
            (w2a[:, :], a["L0_gnn_W2"][0:N, :]), (w2b[0:H - N, :], a["L0_gnn_W2"][N:H, :]),
            (w2b[H - N:H - N + 1, :], row(a["L0_gnn_b2"], F)),
            (nm_in[:, :], a["nodemask"]),
        ]
        loads = [
            (l1w0[0:F, :], a["L1_gnn_W0"]), (l1w0[F:F + 1, :], row(a["L1_gnn_b0"], D1)),
            (l1w1[:, :], a["L1_gnn_W1"]), (l1w2[:, :], a["L1_gnn_W2"]), (l1wo[:, :], a["L1_gnn_Wout"]),
            (l1b1[:, :], spread(a["L1_gnn_b1"], D1)), (l1b2[:, :], spread(a["L1_gnn_b2"], D1)),
            (l1bo[:, :], spread(a["L1_gnn_bout"], F)),
            (l2w[0:F, :], a["L2_gnn_weight"]), (l2w[F:F + 1, :], row(a["L2_gnn_bias"], F)),
            (gamma[:, :], spread(a["L2_gnn_gamma"], F)), (beta[:, :], spread(a["L2_gnn_beta"], F)),
            (l3w1[:, :], a["L3_gnn_W1"]), (l3b1[:, :], a["L3_gnn_b1"].rearrange("(n a) -> n a", a=1)),
            (l3w2[0:F, :], a["L3_gnn_W2"]), (l3w2[F:F + 1, :], row(a["L3_gnn_b2"], F)),
        ]
        ALL_W0 = 16 * len(loads0)
        ALL_W = 16 * len(loads)

        def load_adj(eng, g, p):
            eng.dma_start(adj_in[:, p, :].rearrange("i (b j) -> i b j", j=N), adj_v[:, ds(GS * g, GS), :])\
               .then_inc(s_adj[p], 16)

        def layernorm_std(act, n):
            act.wait_ge(s_var64, n)
            nc.scalar.activation(std[:, :], var[:, :], ACT.Sqrt, bias=eps_col[:, 0:1], scale=1.0 / F)\
              .then_inc(s_std, 1)

        def layernorm_scales(dve, n):
            v = nc.vector
            m0, q0, m1, q1 = (bn6[:, :, k] for k in (1, 2, 4, 5))
            v.tensor_tensor(msum[:, :], m0, m1, ALU.add)
            v.tensor_tensor(dif[:, :], m0, m1, ALU.subtract)
            v.tensor_tensor(var[:, :], q0, q1, ALU.add).then_inc(s_lnstep, 1)
            dve.wait_ge(s_lnstep, 2 * n - 1)
            v.scalar_tensor_tensor(out=dif[:, :], in0=dif[:, :], scalar=F / 4.0, in1=dif[:, :],
                                   op0=ALU.mult, op1=ALU.mult).then_inc(s_lnstep, 1)
            dve.wait_ge(s_lnstep, 2 * n)
            v.tensor_tensor(var[:, :], var[:, :], dif[:, :], ALU.add).then_inc(s_var64, 1)
            dve.wait_ge(s_std, n)
            v.reciprocal(rstd[:, :], std[:, :]).then_inc(s_rstd, 1)
            dve.wait_ge(s_rstd, n)
            v.scalar_tensor_tensor(out=nmr[:, :], in0=msum[:, :], scalar=-0.5, in1=rstd[:, :],
                                   op0=ALU.mult, op1=ALU.mult).then_inc(s_ln, 1)

        def stats(b):
            return nc.vector.bn_stats(bn6[:, ds(b, 1), :].rearrange("p a t -> p (a t)"), x[:, ds(b * F, F)])

        with nc.Block() as block:
            @block.sync
            def _(sp):
                load_adj(sp, 0, 0)
                for n in range(4):
                    sp.dma_start(x3[:, 32 * n:32 * n + 32, :], x_v[:, 32 * n:32 * n + 32, :]).then_inc(s_x[n], 16)
                load_adj(sp, 1, 1)
                for dst, src in loads:
                    sp.dma_start(dst, src).then_inc(s_w, 16)

            @block.gpsimd
            def _(pool):
                g = nc.gpsimd
                g.memset(ident[:, :], 0.0)
                g.memset(ident16[:, :], 0.0)
                g.memset(rankw[:, :], 1.0).then_inc(s_pstep, 1)
                pool.wait_ge(s_pstep, 1)
                for m in (ident, ident16):
                    g.affine_select(out=m[:, :], in_=m[:, :], compare_op=ALU.not_equal, fill=1.0,
                                    base=0, pattern=[[-1, N]], channel_multiplier=1)
                g.affine_select(out=rankw[:, :], in_=rankw[:, :], compare_op=ALU.is_ge, fill=0.0,
                                base=0, pattern=[[1, N]], channel_multiplier=-1).then_inc(s_pstep, 1)
                pool.wait_ge(s_pstep, 2)
                g.affine_select(out=rankw[:, :], in_=rankw[:, :], compare_op=ALU.not_equal, fill=KEY,
                                base=0, pattern=[[-1, N]], channel_multiplier=1)
                g.memset(ones16[:, :], 1.0)
                g.memset(ones[:, :], 1.0)
                g.memset(eps_col[:, :], EPS)
                g.memset(hn[:, :, 0:F], 0.0)
                g.iota(key_i[:, :], pattern=[[SC, MAXC + 1]], base=int(KEY), channel_multiplier=0)\
                 .then_inc(s_const, 1)
                pool.wait_ge(s_wmax, 1)
                g.partition_all_reduce(wmax_all[:, :], wmax[:, :], N, bass.bass_isa.ReduceOp.max)\
                 .then_inc(s_wall, 1)

            @block.scalar
            def _(act):
                for dst, src in loads0:
                    act.dma_start(dst, src).then_inc(s_w0, 16)
                act.wait_ge(s_const, 1)
                layernorm_std(act, 1)

            @block.tensor
            def _(pe):
                pe.wait_ge(s_const, 1)
                pe.wait_ge(s_w0, ALL_W0)
                nc.tensor.transpose(bank[0][:, 0:N], nm_in[:, :], ident[:, :]).then_inc(s_nmT, 1)
                pe.wait_ge(s_nm, 1)
                nc.tensor.matmul(bank[1][:, 0:B], ones[:, :], nm[:, :], start=True, stop=True).then_inc(s_cnt, 1)

            @block.vector
            def _(dve):
                v = nc.vector
                steps = [0]

                def settled(ins):
                    steps[0] += 1
                    ins.then_inc(s_vstep, 1)
                    dve.wait_ge(s_vstep, steps[0])

                v.memset(wmax[:, :], 0.0)
                v.memset(hT0[F:F + 1, :, :], 1.0)
                v.memset(wac[F:F + 1, H:2 * H], 0.0)

                def x_stats(n):
                    dve.wait_ge(s_x[n], 16)
                    for b in range(n * B // 4, (n + 1) * B // 4):
                        last = stats(b)
                    last.then_inc(s_bn, 1)

                x_stats(0)
                x_stats(1)
                dve.wait_ge(s_w0, ALL_W0)
                settled(v.tensor_tensor(wac[0:F, 0:H], w1a[:, :], w1b[:, :], ALU.add))
                v.tensor_copy(wac[0:F, H:2 * H], w1b[:, :])
                settled(v.tensor_scalar(wac[:, 0:H], wac[:, 0:H], -1.0, None, ALU.mult))
                v.tensor_reduce(wmax[0:F + 1, :], wac[:, :], AX.X, ALU.max, apply_absolute_value=True)\
                 .then_inc(s_wmax, 1)
                x_stats(2)
                dve.wait_ge(s_nmT, 1)
                v.tensor_copy(nm[:, :], bank[0][:, 0:B]).then_inc(s_nm, 1)
                dve.wait_ge(s_cnt, 1)
                settled(v.tensor_reduce(cnt_col[:, :], bank[1][:, 0:B], AX.X, ALU.add))
                v.reciprocal(rcnt[:, :], cnt_col[:, :])
                dve.wait_ge(s_wall, 1)
                settled(v.tensor_scalar(wmax_all[:, :], wmax_all[:, :], 2.0 ** -60, None, ALU.max))
                settled(v.tensor_scalar(wexp[:, :].bitcast(I32), wmax_all[:, :].bitcast(I32), 0x7F800000, None,
                                        ALU.bitwise_and))
                v.tensor_scalar(unscale[:, :], wexp[:, :], -(2.0 ** -8), None, ALU.mult)
                settled(v.reciprocal(wscale[:, :], wexp[:, :]))
                settled(v.tensor_scalar(wscale[:, :], wscale[:, :], 2.0 ** 8, None, ALU.mult))
                settled(v.tensor_scalar(wac[:, :], wac[:, :], wscale[0:F + 1, :], None, ALU.mult))
                dve.wait_ge(s_const, 1)
                v.tensor_copy(slot_key[:, :], key_i[:, :])
                x_stats(3)
                dve.wait_ge(s_bn, 4)
                layernorm_scales(dve, 1)

        s_adjTp = sem("adj_transposed")
        s_sg = sem("sign_made")
        s_mask = sem("mask_made")
        s_rank = sem("ranks_made")
        s_rs = sem("ranks_copied")
        s_deg = sem("degree_row_copied")
        s_nop = sem("slot_count_step")
        s_n = sem("slot_counts_ready")
        s_np = sem("padding_counted")
        s_npad = sem("padding_copied")
        s_h = sem("h_normalised")
        s_hTp = sem("h_transposed")
        s_hT = sem("h_transpose_copied")
        s_AC = sem("AC_product_made")
        s_hi = sem("AC_high_part_made")
        s_lo = sem("AC_low_part_made")
        s_acc0 = sem("sum_initialised")
        s_G = sem("onehot_chunk_made")
        s_done = [sem(f"edges_in_bank{k}") for k, _, _ in BANKS]
        s_free = [sem(f"bank{k}_summed") for k, _, _ in BANKS]
        s_half = sem("neighbour_sums_paired")
        s_hm = sem("neighbour_sum_ready")
        s_T = sem("sum_transposed")
        s_hmT = sem("sum_transpose_copied")
        s_W2 = sem("layer0_update_made")
        s_x0 = sem("x_updated_layer0")
        s_bn0 = sem("layer1_stats_made")

        pT, pU = bank[2][:, 0:2 * N], bank[7][:, 0:F]
        pA3, pDeg, pH, pAC, pPad = bank[3], bank[4], bank[4], bank[2], bank[4]

        def known(v):
            return isinstance(v, int)

        def pe_adj(pe, g, p, use):
            pe.wait_ge(s_adj[p], use * 16 + 16)
            pe.wait_ge(s_rs, g)
            pe.wait_ge(s_h, g + 1)
            pe.wait_ge(s_npad, g)
            for q in range(GS):
                last = nc.tensor.transpose(pA3[:, q * N:(q + 1) * N], adj_in[:, p, q * N:(q + 1) * N], ident[:, :])
            last.then_inc(s_adjTp, 1)
            for q in range(GS):
                last = nc.tensor.transpose(pH[0:F, q * N:(q + 1) * N], h0[:, q * F:(q + 1) * F], ident[:, :])
            last.then_inc(s_hTp, 1)

        def pe_rank(pe, g, p):
            pe.wait_ge(s_mask, g + 1)
            pe.wait_ge(s_hT, g + 1)
            nc.tensor.matmul(pA3[:, :], rankw[:, :], mask[:, p, :], start=True, stop=True)
            nc.tensor.matmul(pDeg[0:1, :], ones16[:, 0:1], mask[:, p, :], start=True, stop=True)
            nc.tensor.matmul(pDeg[F:F + 1, :], ones16[:, 0:1], mask[:, p, :], start=True, stop=True)\
              .then_inc(s_rank, 1)

        def pe_pad(pe, g, p):
            pe.wait_ge(s_n, g + 1)
            pe.wait_ge(s_deg, g + 1)
            nc.tensor.matmul(pPad[:, 0:GS], ones16[0:1, :], neg_slots[0:1, :], start=True, stop=False)
            for q in range(GS):
                last = nc.tensor.matmul(pPad[:, q:q + 1], mask[:, p, q * N:(q + 1) * N], ones16[:, 0:1],
                                        start=False, stop=(q == GS - 1))
            last.then_inc(s_np, 1)

        def pe_ac(pe, b, g, p, q):
            pe.wait_ge(s_hT, g + 1)
            pe.wait_ge(s_hi, b)
            if not (known(b) and b < 4):
                pe.wait_ge(s_hmT, b - 3)
            nc.tensor.matmul(pAC[:, 0:2 * H], hT0[:, p, q * N:(q + 1) * N], wac[:, :], start=True, stop=True)\
              .then_inc(s_AC, 1)

        def pe_transpose_sum(pe, b, par):
            pe.wait_ge(s_hm, b + 1)
            if not (known(b) and b + 4 > B):
                pe.wait_ge(s_hi, b + 4)
            else:
                pe.wait_ge(s_hmT, b)
            nc.tensor.transpose(pT[:, 0:N], hm[:, par, 0:N], ident[:, :])
            nc.tensor.transpose(pT[0:H - N, N:2 * N], hm[:, par, N:H], ident[:, :]).then_inc(s_T, 1)

        def pe_update(pe, b, g, p, q):
            pe.wait_ge(s_hmT, b + 1)
            pe.wait_ge(s_deg, g + 1)
            pe.wait_ge(s_x0, b)
            nc.tensor.matmul(pU, hmTa[:, q % 2, :], w2a[:, :], start=True, stop=False)
            nc.tensor.matmul(pU, hmTb[:, p, q * N:(q + 1) * N], w2b[:, :], start=False, stop=True).then_inc(s_W2, 1)

        def pe_chunk(pe, q, c, cnt, prev):
            pe.reg_mov(prev, cnt)
            pe.reg_add(cnt, cnt, 1)
            for k, (n_bank, first, slots) in enumerate(BANKS):
                ps = bank[n_bank]
                pe.wait_ge(s_free[k], prev)
                for e, part in enumerate((ac_hi, ac_lo)):
                    nc.tensor.matmul(ps[:, 0:slots * H].rearrange("p (t h) -> p t h", t=slots), ident16[:, :],
                                     part[:, q, 0:H].unsqueeze(1).broadcast_to([N, slots, H]),
                                     start=(e == 0), stop=False)
                if k == 0:
                    pe.wait_ge(s_G, cnt)
                for t in range(slots):
                    hot = onehot[:, ds(c * (SC * N) + (first + t) * N, N)]
                    for e, part in enumerate((ac_hi, ac_lo)):
                        last = nc.tensor.matmul(ps[:, t * H:(t + 1) * H], hot, part[:, q, H:2 * H],
                                                start=False, stop=(e == 1 and t == slots - 1))
                last.then_inc(s_done[k], 1)

        def pe_slots(pe, b, g, q, cnt, prev, between):
            pe.wait_ge(s_lo, b + 1)
            pe.wait_ge(s_n, g + 1)
            n = pe.value_load(chunks[0:1, ds(b, 1)], min_val=2, max_val=MAXC)
            with pe.Fori(0, n - 1) as c:
                pe_chunk(pe, q, c, cnt, prev)
            between()
            pe_chunk(pe, q, n - 1, cnt, prev)

        def around(i, body, *more):
            for u in range(2):
                g = 2 * i + u
                for q in range(GS):
                    nxt = None if known(g) and g == NG - 1 else g + 1
                    body(8 * i + 4 * u + q, g, u, q, nxt, 1 - u, i if u == 0 else i + 1)

        def all_iterations(eng, body):
            around(0, body)
            with eng.Fori(1, NI - 1) as i:
                around(i, body)
            around(NI - 1, body)

        def group_of(b, g, u, q, back):
            r = q - back
            if 0 <= r < GS:
                return g, u, r
            return (g - 1, 1 - u, r + GS) if r < 0 else (g + 1, 1 - u, r - GS)

        def act_adj(act, g, p):
            act.wait_ge(s_adjTp, g + 1)
            nc.scalar.activation(adjT[:, ds(g * (GS * N), GS * N)], pA3[:, :], ACT.Copy)
            nc.scalar.activation(sgn[:, :], pA3[:, :], ACT.Sign).then_inc(s_sg, 1)
            act.wait_ge(s_sg, g + 1)
            nc.scalar.activation(mask[:, p, :], sgn[:, :], ACT.Relu).then_inc(s_mask, 1)
            act.wait_ge(s_hTp, g + 1)
            nc.scalar.activation(hT0[0:F, p, :], pH[0:F, :], ACT.Copy).then_inc(s_hT, 1)

        def act_h(act, g):
            act.wait_ge(s_hTp, g)
            for q in range(GS):
                last = nc.scalar.activation(h0[:, q * F:(q + 1) * F], x[:, ds((g * GS + q) * F, F)], ACT.Relu,
                                            bias=nmr[:, ds(g * GS + q, 1)], scale=rstd[:, ds(g * GS + q, 1)])
            last.then_inc(s_h, 1)

        def act_rank(act, g, p):
            act.wait_ge(s_rank, g + 1)
            for t in range(SC):
                last = nc.scalar.activation(rs[:, p, :, t, :], pA3[:, :].rearrange("p (q j) -> p q j", q=GS),
                                            ACT.Copy, bias=-float(t))
            last.then_inc(s_rs, 1)

        def act_pad(act, g, p):
            act.wait_ge(s_np, g + 1)
            nc.scalar.activation(neg_pad[:, p, :], pPad[:, 0:GS], ACT.Copy, scale=0.25).then_inc(s_npad, 1)

        def act_degrees(act, g, p, updates):
            act.wait_ge(s_rank, g + 1)
            if updates is not None:
                act.wait_ge(s_W2, updates)
            nc.scalar.activation(hmTb[F:F + 1, p, :], pDeg[F:F + 1, :], ACT.Copy).then_inc(s_deg, 1)

        def act_ac(act, b, q):
            act.wait_ge(s_AC, b + 1)
            if not (known(b) and b < 2):
                act.wait_ge(s_lo, b - 1)
                act.wait_ge(s_acc0, b - 1)
            nc.scalar.activation(ac32[:, q % 2, :], pAC[:, 0:2 * H], ACT.Copy)
            nc.scalar.activation(ac_hi[:, q, :], pAC[:, 0:2 * H], ACT.Copy).then_inc(s_hi, 1)

        def act_init(act, b, g, p, q):
            act.wait_ge(s_npad, g + 1)
            act.wait_ge(s_hi, b + 1)
            if not (known(b) and b < 4):
                act.wait_ge(s_hm, b - 3)
            nc.scalar.activation(acc[:, q, :].rearrange("p (t h) -> p t h", t=4),
                                 ac32[:, q % 2, 0:H].unsqueeze(1).broadcast_to([N, 4, H]), ACT.Relu,
                                 scale=neg_pad[:, p, q:q + 1]).then_inc(s_acc0, 1)

        def act_sum(act, b, p, q):
            act.wait_ge(s_T, b + 1)
            nc.scalar.activation(hmTa[:, q % 2, :], pT[:, 0:N], ACT.Copy, scale=unscale[:, 0:1])
            nc.scalar.activation(hmTb[0:H - N, p, q * N:(q + 1) * N], pT[0:H - N, N:2 * N], ACT.Copy,
                                 scale=unscale[0:H - N, 0:1]).then_inc(s_hmT, 1)

        def dve_counts(dve, g):
            dve.wait_ge(s_rank, g + 1)
            nc.vector.tensor_reduce(maxdeg[:, :], pDeg[0:1, :].rearrange("p (q j) -> p q j", q=GS), AX.X, ALU.max)\
              .then_inc(s_nop, 1)
            dve.wait_ge(s_nop, 4 * g + 1)
            nc.vector.tensor_scalar(maxdeg[:, :], maxdeg[:, :], float(SC + 1), float(SC - 1), ALU.max, ALU.add)\
              .then_inc(s_nop, 1)
            dve.wait_ge(s_nop, 4 * g + 2)
            nc.vector.tensor_scalar(maxdeg_i[:, :], maxdeg[:, :], float(DIV), None, ALU.mult).then_inc(s_nop, 1)
            dve.wait_ge(s_nop, 4 * g + 3)
            nc.vector.tensor_scalar(chunks[:, ds(g * GS, GS)], maxdeg_i[:, :], SH, None, ALU.arith_shift_right)\
              .then_inc(s_nop, 1)
            dve.wait_ge(s_nop, 4 * g + 4)
            if not (known(g) and g == 0):
                dve.wait_ge(s_np, g)
            nc.vector.tensor_scalar(neg_slots[:, :], chunks[:, ds(g * GS, GS)], -float(SC), None, ALU.mult)\
              .then_inc(s_n, 1)

        def dve_onehot(p, q, c):
            nc.vector.tensor_scalar(onehot[:, ds(c * (SC * N), SC * N)],
                                    rs[:, p, q, :, :].rearrange("p t j -> p (t j)"),
                                    slot_key[:, ds(c, 1)], None, ALU.is_equal).then_inc(s_G, 1)

        def dve_slots(dve, b, g, u, q, cnt, prev):
            dve.wait_ge(s_acc0, b + 1)
            dve.wait_ge(s_n, g + 1)
            n = dve.value_load(chunks[0:1, ds(b, 1)], min_val=2, max_val=MAXC)

            def chunk():
                for k, (n_bank, _, slots) in enumerate(BANKS):
                    sums = acc[:, q, (k % 2) * 2 * H:(k % 2) * 2 * H + slots * H]
                    dve.wait_ge(s_done[k], cnt)
                    if k < 2:
                        dve.wait_ge(s_free[k + 2], prev)
                    else:
                        dve.wait_ge(s_free[k - 2], cnt)
                    nc.vector.scalar_tensor_tensor(out=sums, in0=bank[n_bank][:, 0:slots * H], scalar=0.0, in1=sums,
                                                   op0=ALU.min, op1=ALU.add).then_inc(s_free[k], 1)

            with dve.Fori(0, n - 1) as c:
                dve.reg_mov(prev, cnt)
                dve.reg_add(cnt, cnt, 1)
                dve_onehot(u, q, c + 1)
                chunk()
            dve.reg_mov(prev, cnt)
            dve.reg_add(cnt, cnt, 1)
            if not (known(b) and b == B - 1):
                g1, p1, q1 = group_of(b, g, u, q, -1)
                dve.wait_ge(s_rs, g1 + 1)
                dve_onehot(p1, q1, 0)
            chunk()

        def dve_update(dve, b):
            xb = x[:, ds(b * F, F)]
            dve.wait_ge(s_x0, b)
            dve.wait_ge(s_W2, b + 1)
            nc.vector.tensor_tensor(xb, pU, xb, ALU.add).then_inc(s_x0, 1)
            if not (known(b) and b == 0):
                stats(b - 1)

        def pool_low(pool, b, q):
            pool.wait_ge(s_hi, b + 1)
            nc.gpsimd.tensor_tensor(ac_lo[:, q, :], ac32[:, q % 2, :], ac_hi[:, q, :], ALU.subtract)\
              .then_inc(s_lo, 1)

        def pool_sum(pool, b, g, q, total):
            pool.wait_ge(s_n, g + 1)
            n = pool.value_load(chunks[0:1, ds(b, 1)], min_val=2, max_val=MAXC)
            pool.reg_add(total, total, n)
            for k in range(len(BANKS)):
                pool.wait_ge(s_free[k], total)
            nc.gpsimd.tensor_tensor(acc[:, q, 0:2 * H], acc[:, q, 0:2 * H], acc[:, q, 2 * H:4 * H], ALU.add)\
              .then_inc(s_half, 1)
            pool.wait_ge(s_half, b + 1)
            nc.gpsimd.tensor_tensor(hm[:, q % 2, :], acc[:, q, 0:H], acc[:, q, H:2 * H], ALU.add).then_inc(s_hm, 1)

        with nc.Block() as block:
            @block.sync
            def _(sp):
                with sp.Fori(1, NI) as i:
                    for p in range(2):
                        sp.wait_ge(s_adjTp, 2 * i + p - 1)
                        load_adj(sp, 2 * i + p, p)

            @block.tensor
            def _(pe):
                cnt, prev = pe.alloc_register("pe_chunk"), pe.alloc_register("pe_chunk_before")
                pe.reg_mov(cnt, 0)
                pe_adj(pe, 0, 0, 0)
                pe_rank(pe, 0, 0)
                pe_pad(pe, 0, 0)
                pe_ac(pe, 0, 0, 0, 0)
                pe_ac(pe, 1, 0, 0, 1)

                def step(b, g, u, q, nxt, p, use):
                    if nxt is not None:
                        if q == 0:
                            pe_adj(pe, nxt, p, use)
                        if q == 1:
                            pe_rank(pe, nxt, p)
                        if q == 3:
                            pe_pad(pe, nxt, p)
                    if not (known(b) and b + 2 >= B):
                        pe_ac(pe, b + 2, *group_of(b, g, u, q, -2))

                    def between():
                        if not (known(b) and b < 1):
                            pe_transpose_sum(pe, b - 1, (q - 1) % 2)
                        if not (known(b) and b < 2):
                            pe_update(pe, b - 2, *group_of(b, g, u, q, 2))

                    pe_slots(pe, b, g, q, cnt, prev, between)

                all_iterations(pe, step)
                pe_transpose_sum(pe, B - 1, 1)
                pe_update(pe, B - 2, NG - 1, 1, 2)
                pe_update(pe, B - 1, NG - 1, 1, 3)

            @block.scalar
            def _(act):
                act_h(act, 0)
                act_adj(act, 0, 0)
                act_h(act, 1)
                act_rank(act, 0, 0)
                act_degrees(act, 0, 0, None)
                act_pad(act, 0, 0)
                act_ac(act, 0, 0)
                act_ac(act, 1, 1)
                act_init(act, 0, 0, 0, 0)

                def step(b, g, u, q, nxt, p, use):
                    if nxt is not None:
                        if q == 0:
                            act_adj(act, nxt, p)
                        if q == 1:
                            act_rank(act, nxt, p)
                        if q == 3:
                            act_degrees(act, nxt, p, None if known(nxt) and nxt < 2 else GS * nxt - GS)
                    if not (known(b) and b + 2 >= B):
                        act_ac(act, b + 2, (q + 2) % GS)
                    if nxt is not None and q == 3:
                        act_pad(act, nxt, p)
                    if not (known(b) and b + 1 >= B):
                        act_init(act, b + 1, *group_of(b, g, u, q, -1))
                    if q == 1 and not (known(g) and g + 2 >= NG):
                        act_h(act, g + 2)
                    if not (known(b) and b < 1):
                        act_sum(act, b - 1, *group_of(b, g, u, q, 1)[1:])

                all_iterations(act, step)
                act_sum(act, B - 1, 1, 3)

            @block.vector
            def _(dve):
                cnt, prev = dve.alloc_register("dve_chunk"), dve.alloc_register("dve_chunk_before")
                dve.reg_mov(cnt, 0)
                dve_counts(dve, 0)
                dve.wait_ge(s_rs, 1)
                dve_onehot(0, 0, 0)

                def step(b, g, u, q, nxt, p, use):
                    if nxt is not None and q == 2:
                        dve_counts(dve, nxt)
                    dve_slots(dve, b, g, u, q, cnt, prev)
                    if not (known(b) and b < 2):
                        dve_update(dve, b - 2)

                all_iterations(dve, step)
                for b in range(B - 2, B):
                    dve_update(dve, b)
                dve.wait_ge(s_x0, B)
                stats(B - 1).then_inc(s_bn0, 1)

            @block.gpsimd
            def _(pool):
                total = pool.alloc_register("pool_chunks")
                pool.reg_mov(total, 0)
                pool_low(pool, 0, 0)
                pool_low(pool, 1, 1)

                def step(b, g, u, q, nxt, p, use):
                    if not (known(b) and b + 2 >= B):
                        pool_low(pool, b + 2, (q + 2) % GS)
                    pool_sum(pool, b, g, q, total)

                all_iterations(pool, step)

        s_hn1 = [sem(f"l1_h_normalised{u}") for u in range(2)]
        s_p1 = [sem(f"l1_stage_done{u}") for u in range(2)]
        s_c1 = [sem(f"l1_stage_copied{u}") for u in range(2)]
        s_t1 = [sem(f"l1_update_step{u}") for u in range(2)]
        s_bn1 = sem("layer2_stats_made")
        ST = 8

        def norm_graph(s_done, u, b, q, last):
            ins = nc.scalar.activation(hn[:, u, (q + 1) * F:(q + 2) * F], x[:, ds((b + q) * F, F)], ACT.Relu,
                                       bias=nmr[:, ds(b + q, 1)], scale=rstd[:, ds(b + q, 1)])
            if last:
                ins.then_inc(s_done, 1)

        def grp(u, i):
            return 2 * i + u

        with nc.Block() as block:
            @block.tensor
            def _(pe):
                turn = [pe.alloc_register(f"l1_turn{u}") for u in range(2)]
                for u in range(2):
                    pe.reg_mov(turn[u], 1)
                pe.wait_ge(s_w, ALL_W)
                with pe.Fori(0, NI) as i:
                    for st in range(ST):
                        for u in range(2):
                            ps = bank[4 * u + (st % 2)]
                            b0 = GS * grp(u, i)
                            pe.wait_ge(s_c1[u], ST * i + st)
                            if st == 0:
                                pe.wait_ge(s_hn1[u], turn[u])
                                pe.reg_add(turn[u], turn[u], 1)
                            for q in range(GS):
                                cols = slice(q * N, (q + 1) * N)
                                if st == 0:
                                    last = nc.tensor.transpose(ps[0:F, cols], hn[:, u, (q + 1) * F:(q + 2) * F], ident[:, :])
                                elif st == 1:
                                    last = nc.tensor.matmul(ps[:, cols], hT[:, u, cols], l1w0[:, :], start=True, stop=True)
                                elif st in (2, 4, 6):
                                    last = nc.tensor.matmul(ps[:, cols], msg[:, u, cols],
                                                            adjT[:, ds((b0 + q) * N, N)], start=True, stop=True)
                                elif st in (3, 5):
                                    w = l1w1 if st == 3 else l1w2
                                    last = nc.tensor.matmul(ps[:, cols], hid[:, u, cols], w[:, :], start=True, stop=True)
                                else:
                                    last = nc.tensor.matmul(ps[:, q * F:(q + 1) * F], hid[:, u, cols], l1wo[:, :],
                                                            start=True, stop=True)
                            last.then_inc(s_p1[u], 1)

            @block.scalar
            def _(act):
                layernorm_std(act, 2)
                act.wait_ge(s_ln, 2)
                for u in range(2):
                    for q in range(GS):
                        norm_graph(s_hn1[u], u, GS * u, q, q == GS - 1)

                def group_pair(i, more):
                    for st in range(ST):
                        for u in range(2):
                            if st in (0, 2, 4, 6):
                                act.wait_ge(s_p1[u], ST * i + st + 1)
                            ps = bank[4 * u + (st % 2)]
                            if st == 0:
                                nc.scalar.activation(hT[0:F, u, :], ps[0:F, :], ACT.Copy).then_inc(s_c1[u], 1)
                            elif st in (2, 4, 6):
                                nc.scalar.activation(hid[:, u, :], ps[:, :], ACT.Relu).then_inc(s_c1[u], 1)
                            elif more:
                                q = st // 2
                                norm_graph(s_hn1[u], u, GS * grp(u, i + 1), q, q == GS - 1)

                with act.Fori(0, NI - 1) as i:
                    group_pair(i, True)
                group_pair(NI - 1, False)

            @block.vector
            def _(dve):
                dve.wait_ge(s_bn0, 1)
                layernorm_scales(dve, 2)

                dve.wait_ge(s_w, ALL_W)

                def pair_stats(i, first, count):
                    for e in range(first, first + count):
                        last = stats(2 * GS * i + e)
                    return last

                def group_pair(i, before):
                    for st in (1, 3, 5):
                        for u in range(2):
                            ps = bank[4 * u + (st % 2)]
                            dve.wait_ge(s_p1[u], ST * i + st + 1)
                            if st == 1:
                                nc.vector.tensor_copy(msg[:, u, :], ps[:, :]).then_inc(s_c1[u], 1)
                            else:
                                bias = l1b1 if st == 3 else l1b2
                                nc.vector.tensor_tensor(
                                    msg[:, u, :].rearrange("p (q d) -> p q d", q=GS),
                                    ps[:, :].rearrange("p (q d) -> p q d", q=GS),
                                    bias[:, :].unsqueeze(1).broadcast_to([N, GS, D1]), ALU.add).then_inc(s_c1[u], 1)
                        if before is not None:
                            if st == 1:
                                for u in range(2):
                                    dve.wait_ge(s_t1[u], 2 * i)
                            last = pair_stats(before, {1: 0, 3: 3, 5: 6}[st], {1: 3, 3: 3, 5: 2}[st])
                            if st == 5:
                                last.then_inc(s_bn1, 1)
                    up3 = [upd[:, u, :].rearrange("p (q f) -> p q f", q=GS) for u in range(2)]
                    for u in range(2):
                        dve.wait_ge(s_p1[u], ST * i + ST)
                        nc.vector.tensor_tensor(up3[u], bank[4 * u + 1][:, 0:GS * F].rearrange("p (q f) -> p q f", q=GS),
                                                l1bo[:, :].unsqueeze(1).broadcast_to([N, GS, F]), ALU.add)\
                          .then_inc(s_c1[u], 1)
                    for u in range(2):
                        dve.wait_ge(s_c1[u], ST * i + ST)
                        nc.vector.tensor_tensor(up3[u], up3[u],
                                                nm[:, ds(GS * grp(u, i), GS)].unsqueeze(2).broadcast_to([N, GS, F]),
                                                ALU.mult).then_inc(s_t1[u], 1)
                    for u in range(2):
                        xg = x[:, ds(GS * grp(u, i) * F, GS * F)]
                        dve.wait_ge(s_t1[u], 2 * i + 1)
                        nc.vector.tensor_tensor(xg, xg, upd[:, u, :], ALU.add).then_inc(s_t1[u], 1)

                group_pair(0, None)
                with dve.Fori(1, NI) as i:
                    group_pair(i, i - 1)
                for u in range(2):
                    dve.wait_ge(s_t1[u], 2 * NI)
                pair_stats(NI - 1, 0, 2 * GS).then_inc(s_bn1, 1)

        s_hn2 = [sem(f"l2_h_normalised{u}") for u in range(2)]
        s_p2 = [sem(f"l2_stage_done{u}") for u in range(2)]
        s_c2 = [sem(f"l2_stage_copied{u}") for u in range(2)]
        s_q2 = [sem(f"l2_squares_made{u}") for u in range(2)]
        s_n2 = [sem(f"l2_row_sums_made{u}") for u in range(2)]

        with nc.Block() as block:
            @block.tensor
            def _(pe):
                with pe.Fori(0, NI) as i:
                    for st in range(2):
                        for u in range(2):
                            ps = bank[4 * u + st]
                            b0 = GS * grp(u, i)
                            pe.wait_ge(s_c2[u], 2 * i + st)
                            if st == 0:
                                pe.wait_ge(s_hn2[u], i + 1)
                            for q in range(GS):
                                cols = slice(q * N, (q + 1) * N)
                                if st == 0:
                                    hq = hn[:, u, (q + 1) * F:(q + 2) * F]
                                    nc.tensor.matmul(ps[0:F, cols], hq, adjT[:, ds((b0 + q) * N, N)],
                                                     start=True, stop=False)
                                    last = nc.tensor.matmul(ps[0:F, cols], hq, ident[:, :], start=False, stop=True)
                                else:
                                    last = nc.tensor.matmul(ps[:, q * F:(q + 1) * F], hT[:, u, cols], l2w[:, :],
                                                            start=True, stop=True)
                            last.then_inc(s_p2[u], 1)

            @block.scalar
            def _(act):
                layernorm_std(act, 3)
                act.wait_ge(s_ln, 3)
                for u in range(2):
                    for q in range(GS):
                        norm_graph(s_hn2[u], u, GS * u, q, q == GS - 1)

                def group_pair(i, more):
                    if more:
                        for u in range(2):
                            act.wait_ge(s_p2[u], 2 * i + 1)
                            for q in range(GS):
                                norm_graph(s_hn2[u], u, GS * grp(u, i + 1), q, q == GS - 1)
                    for u in range(2):
                        b0 = GS * grp(u, i)
                        act.wait_ge(s_p2[u], 2 * i + 2)
                        nc.scalar.activation(y[:, ds(b0 * F, GS * F)], bank[4 * u + 1][:, 0:GS * F], ACT.Copy)
                        act.wait_ge(s_n2[u], i)
                        nc.scalar.activation(upd[:, u, :], bank[4 * u + 1][:, 0:GS * F], ACT.Square)\
                          .then_inc(s_c2[u], 1)

                with act.Fori(0, NI - 1) as i:
                    group_pair(i, True)
                group_pair(NI - 1, False)

            @block.vector
            def _(dve):
                dve.wait_ge(s_bn1, NI)
                layernorm_scales(dve, 3)
                with dve.Fori(0, NI) as i:
                    for u in range(2):
                        dve.wait_ge(s_p2[u], 2 * i + 1)
                        nc.vector.tensor_copy(hT[0:F, u, :], bank[4 * u][0:F, :]).then_inc(s_c2[u], 1)
                    for u in range(2):
                        dve.wait_ge(s_c2[u], 2 * i + 2)
                        nc.vector.tensor_reduce(ss[:, ds(GS * grp(u, i), GS)],
                                                upd[:, u, :].rearrange("p (q f) -> p q f", q=GS), AX.X, ALU.add)\
                          .then_inc(s_n2[u], 1)

        s_nrm = sem("row_norms_ready")
        s_y = sem("y_chunk_normalised")
        s_ym = sem("y_chunk_masked")
        s_yms = sem("y_masked_chunk_summed")
        s_vb = sem("batchnorm_step")
        s_mean = sem("batchnorm_mean_ready")
        s_d = sem("y_chunk_centred")
        s_dq = sem("y_chunk_squared")
        s_dm = sem("y_square_masked")
        s_dms = sem("y_square_chunk_summed")
        s_var = sem("batchnorm_std_ready")
        s_ya = sem("y_chunk_scaled")
        s_yb = sem("y_chunk_shifted")
        s_yc = sem("y_chunk_shifted_masked")
        s_xn = sem("x_updated_layer2")
        s_bn2 = sem("layer3_stats_made")

        def yc(c):
            return y[:, ds(c * XC, XC)]

        def g3(ap):
            return ap.rearrange("p (g f) -> p g f", f=F)

        def per_graph(t, c):
            return t[:, ds(c * GX, GX)].unsqueeze(2).broadcast_to([N, GX, F])

        def per_feature(t):
            return t.unsqueeze(1).broadcast_to([N, GX, F])

        with nc.Block() as block:
            @block.tensor
            def _(pe):
                def add(ps, k, src, ready, done, first, last):
                    pe.wait_ge(ready, k + 1)
                    nc.tensor.matmul(ps[:, :], ones[:, :], src, start=first, stop=last).then_inc(done, 1)

                for ps, off, ready, done in ((bank[0], 0, s_ym, s_yms), (bank[1], 2, s_dm, s_dms)):
                    add(ps, 0, tmp[:, off, :], ready, done, True, False)
                    for k in range(1, NXC):
                        add(ps, k, tmp[:, off + k % 2, :], ready, done, False, k == NXC - 1)

            @block.vector
            def _(dve):
                v = nc.vector
                steps = [0]

                def settled(ins):
                    steps[0] += 1
                    ins.then_inc(s_vb, 1)
                    dve.wait_ge(s_vb, steps[0])

                dve.wait_ge(s_nrm, 1)
                settled(v.tensor_scalar(ss[:, :], ss[:, :], 1e-12, None, ALU.max))
                settled(v.reciprocal(ss[:, :], ss[:, :]))
                with dve.Fori(0, NXC) as c:
                    v.tensor_tensor(g3(yc(c)), g3(yc(c)), per_graph(ss, c), ALU.mult).then_inc(s_y, 1)
                dve.wait_ge(s_yms, NXC)
                settled(v.tensor_reduce(stat[:, 0, :], bank[0][:, :].rearrange("p (g f) -> p f g", f=F), AX.X, ALU.add))
                v.tensor_scalar(stat[:, 1, :], stat[:, 0, :], rcnt[:, :], None, ALU.mult).then_inc(s_mean, 1)
                dve.wait_ge(s_mean, 1)
                with dve.Fori(0, NXC) as c:
                    v.tensor_tensor(g3(yc(c)), g3(yc(c)), per_feature(stat[:, 1, :]), ALU.subtract).then_inc(s_d, 1)
                dve.wait_ge(s_dms, NXC)
                settled(v.tensor_reduce(stat[:, 2, :], bank[1][:, :].rearrange("p (g f) -> p f g", f=F), AX.X, ALU.add))
                settled(v.tensor_scalar(stat[:, 3, :], stat[:, 2, :], rcnt[:, :], None, ALU.mult))
                dve.wait_ge(s_var, 1)
                settled(v.reciprocal(stat[:, 5, :], stat[:, 4, :]))
                settled(v.tensor_tensor(stat[:, 5, :], stat[:, 5, :], gamma[:, :], ALU.mult))
                with dve.Fori(0, NXC) as c:
                    v.tensor_tensor(g3(yc(c)), g3(yc(c)), per_feature(stat[:, 5, :]), ALU.mult).then_inc(s_ya, 1)
                with dve.Fori(0, NXC) as c:
                    xc = x[:, ds(c * XC, XC)]
                    dve.wait_ge(s_yc, c + 1)
                    v.scalar_tensor_tensor(out=xc, in0=yc(c), scalar=0.0, in1=xc, op0=ALU.max, op1=ALU.add)\
                     .then_inc(s_xn, 1)
                    dve.wait_ge(s_xn, c + 1)
                    for e in range(GX):
                        last = stats(c * GX + e)
                    last.then_inc(s_bn2, 1)
                dve.wait_ge(s_bn2, NXC)
                layernorm_scales(dve, 4)

            @block.scalar
            def _(act):
                act.activation(ss[:, :], ss[:, :], ACT.Sqrt).then_inc(s_nrm, 1)
                for c in range(NXC):
                    act.wait_ge(s_d, c + 1)
                    if c >= 2:
                        act.wait_ge(s_dms, c - 1)
                    act.activation(tmp[:, 2 + c % 2, :], yc(c), ACT.Square).then_inc(s_dq, 1)
                act.wait_ge(s_vb, 5)
                act.activation(stat[:, 4, :], stat[:, 3, :], ACT.Sqrt, bias=eps_col[:, 0:1]).then_inc(s_var, 1)
                layernorm_std(act, 4)

            @block.gpsimd
            def _(pool):
                g = nc.gpsimd
                for c in range(NXC):
                    pool.wait_ge(s_y, c + 1)
                    if c >= 2:
                        pool.wait_ge(s_yms, c - 1)
                    g.tensor_tensor(g3(tmp[:, c % 2, :]), g3(yc(c)), per_graph(nm, c), ALU.mult).then_inc(s_ym, 1)
                for c in range(NXC):
                    pool.wait_ge(s_dq, c + 1)
                    t = g3(tmp[:, 2 + c % 2, :])
                    g.tensor_tensor(t, t, per_graph(nm, c), ALU.mult).then_inc(s_dm, 1)
                with pool.Fori(0, NXC) as c:
                    pool.wait_ge(s_ya, c + 1)
                    g.tensor_tensor(g3(yc(c)), g3(yc(c)), per_feature(beta[:, :]), ALU.add).then_inc(s_yb, 1)
                    pool.wait_ge(s_yb, c + 1)
                    g.tensor_tensor(g3(yc(c)), g3(yc(c)), per_graph(nm, c), ALU.mult).then_inc(s_yc, 1)

        s_hn3 = [sem(f"l3_h_normalised{u}") for u in range(2)]
        s_p3 = [sem(f"l3_stage_done{u}") for u in range(2)]
        s_c3 = [sem(f"l3_stage_copied{u}") for u in range(2)]
        s_out = [sem(f"stored{u}") for u in range(2)]

        with nc.Block() as block:
            @block.tensor
            def _(pe):
                with pe.Fori(0, NI) as i:
                    for st in range(3):
                        for u in range(2):
                            ps = bank[4 * u + st]
                            b0 = GS * grp(u, i)
                            pe.wait_ge(s_c3[u], 3 * i + st)
                            if st == 0:
                                pe.wait_ge(s_hn3[u], i + 1)
                                for q in range(GS):
                                    cols = slice(q * N, (q + 1) * N)
                                    hq = hn[:, u, (q + 1) * F:(q + 2) * F]
                                    nc.tensor.matmul(ps[:, cols], hn[:, u, q * F:(q + 2) * F],
                                                     adjT[:, ds((b0 + q) * N, N)], start=True, stop=True)
                                    last = nc.tensor.transpose(ps[0:F, cols], hq, ident[:, :])
                            elif st == 1:
                                last = nc.tensor.matmul(ps[0:F, :], l3w1[:, :], msg[:, u, :], start=True, stop=True)
                            else:
                                for q in range(GS):
                                    cols = slice(q * N, (q + 1) * N)
                                    last = nc.tensor.matmul(ps[:, q * F:(q + 1) * F], hT[:, u, cols], l3w2[:, :],
                                                            start=True, stop=True)
                            last.then_inc(s_p3[u], 1)

            @block.scalar
            def _(act):
                nc.scalar.activation(std[:, 0:1], eps_col[:, 0:1], ACT.Tanh)
                act.wait_ge(s_ln, 4)
                for u in range(2):
                    for q in range(GS):
                        norm_graph(s_hn3[u], u, GS * u, q, q == GS - 1)

                def group_pair(i, more):
                    for u in range(2):
                        act.wait_ge(s_p3[u], 3 * i + 2)
                        nc.scalar.activation(hT[0:F, u, :], bank[4 * u + 1][0:F, :], ACT.Tanh, bias=l3b1[:, 0:1])\
                          .then_inc(s_c3[u], 1)
                        if more:
                            for q in range(GS):
                                norm_graph(s_hn3[u], u, GS * grp(u, i + 1), q, q == GS - 1)

                with act.Fori(0, NI - 1) as i:
                    group_pair(i, True)
                group_pair(NI - 1, False)

            @block.vector
            def _(dve):
                with dve.Fori(0, NI) as i:
                    for u in range(2):
                        dve.wait_ge(s_p3[u], 3 * i + 1)
                        nc.vector.tensor_copy(msg[:, u, :], bank[4 * u][:, :]).then_inc(s_c3[u], 1)
                    for u in range(2):
                        dve.wait_ge(s_p3[u], 3 * i + 3)
                        dve.wait_ge(s_out[u], 16 * i)
                        nc.vector.tensor_tensor(upd[:, u, :], bank[4 * u + 2][:, 0:GS * F],
                                                x[:, ds(GS * grp(u, i) * F, GS * F)], ALU.add).then_inc(s_c3[u], 1)

            @block.sync
            def _(sp):
                with sp.Fori(0, NI) as i:
                    for u in range(2):
                        sp.wait_ge(s_c3[u], 3 * i + 3)
                        sp.dma_start(out_v[:, ds(GS * grp(u, i), GS), :],
                                     upd[:, u, :].rearrange("p (q f) -> p q f", q=GS)).then_inc(s_out[u], 16)
                for u in range(2):
                    sp.wait_ge(s_out[u], 16 * NI)


_INS = ["x", "adj", "nodemask", "L0_gnn_W1", "L0_gnn_b1", "L0_gnn_W2", "L0_gnn_b2",
        "L1_gnn_W0", "L1_gnn_b0", "L1_gnn_W1", "L1_gnn_b1", "L1_gnn_W2", "L1_gnn_b2",
        "L1_gnn_Wout", "L1_gnn_bout", "L2_gnn_weight", "L2_gnn_bias", "L2_gnn_gamma",
        "L2_gnn_beta", "L3_gnn_W1", "L3_gnn_b1", "L3_gnn_W2", "L3_gnn_b2"]
_OUTS = [((128, 128, 64), "float32")]


def kernel(**inputs):
    import numpy as _np
    import concourse.bacc as _bacc
    from concourse import mybir as _mybir
    from concourse.bass_utils import run_bass_kernel_spmd as _run

    nc = _bacc.Bacc("TRN2", target_bir_lowering=False, num_devices=1)
    arrays, args = {}, {}
    for name in _INS:
        v = _np.ascontiguousarray(inputs[name])
        arrays[f"in_{name}_dram"] = v
        args[name] = nc.dram_tensor(f"in_{name}_dram", v.shape, _mybir.dt.from_np(v.dtype), kind="ExternalInput").ap()
    outs = [nc.dram_tensor(f"out_{i}_dram", s, _mybir.dt.from_np(_np.dtype(d)), kind="ExternalOutput").ap()
            for i, (s, d) in enumerate(_OUTS)]
    gnn_stack_kernel(nc, args, outs[0])
    r = _run(nc, [arrays], core_ids=[0])
    return r.results[0]["out_0_dram"]
```

```python
import concourse.bass as bass
from concourse import mybir
from contextlib import ExitStack

F32 = mybir.dt.float32
F16 = mybir.dt.float16
I32 = mybir.dt.int32
ALU = mybir.AluOpType
ACT = mybir.ActivationFunctionType
AX = mybir.AxisListType


def gnn_stack_kernel(nc, a, out):
    B, N, F = a["x"].shape
    H = a["L0_gnn_W2"].shape[0]
    D1 = a["L1_gnn_W0"].shape[1]
    GS = 4
    NG = B // GS
    NI = NG // 2
    OWN = [(0, 0, 0, 2), (1, 1, 2, 2), (2, 5, 4, 2), (3, 6, 6, 1)]
    SHARED = [(0, 0, 0, 2), (1, 1, 2, 2), (3, 6, 4, 1)]
    SC = 7
    SS = 5
    MAXR = -(-N // SC)
    MINC = 2
    NC = MAXR - MINC - 1
    MAXC = MAXR
    DIV, SH = 13108, 16
    RING = 4
    EPS = 1e-5
    KEY = 257.0
    XC = 512
    NXC = B * F // XC
    GX = XC // F

    ctx = ExitStack()
    with ctx:
        def sb(name, shape, dt=F32):
            return ctx.enter_context(nc.sbuf_tensor(name, shape, dt))

        def sem(name):
            return ctx.enter_context(nc.semaphore(name))

        x = sb("x_all", [N, B * F])
        adjT = sb("adjT_all", [N, B * N])
        ident = sb("ident", [N, N])
        ident16 = sb("ident16", [N, N], F16)
        rankw = sb("rankw", [N, N], F16)
        ones16 = sb("ones16", [N, N], F16)
        ones = sb("ones", [N, N])
        key_i = sb("key_i", [N, MAXC + 1], I32)
        slot_key = sb("slot_key", [N, MAXC + 1])
        before16 = sb("before16", [N, N], F16)
        row_i = sb("row_i", [N, N], I32)
        row_f = sb("row_f", [N, N])
        row_slots = sb("row_slots", [1, N], F16)
        cand_i = sb("cand_i", [N, NC], I32)
        cand = sb("cand", [N, NC])
        eps_col = sb("eps_col", [N, 1])
        w1a = sb("w1a", [F, H])
        w1b = sb("w1b", [F, H])
        wac = sb("wac", [F + 1, 2 * H])
        wmax = sb("wmax", [N, 1])
        wmax_all = sb("wmax_all", [N, 1])
        wexp = sb("wexp", [N, 1])
        wscale = sb("wscale", [N, 1])
        unscale = sb("unscale", [N, 1])
        w2a = sb("w2a", [N, F])
        w2b = sb("w2b", [H - N + 1, F])
        l1w0 = sb("l1w0", [F + 1, D1])
        l1w1 = sb("l1w1", [D1, D1])
        l1w2 = sb("l1w2", [D1, D1])
        l1wo = sb("l1wo", [D1, F])
        l1b1 = sb("l1b1", [N, D1])
        l1b2 = sb("l1b2", [N, D1])
        l1bo = sb("l1bo", [N, F])
        l2w = sb("l2w", [F + 1, F])
        gamma = sb("gamma", [N, F])
        beta = sb("beta", [N, F])
        l3w1 = sb("l3w1", [2 * F, F])
        l3b1 = sb("l3b1", [F, 1])
        l3w2 = sb("l3w2", [F + 1, F])
        nm_in = sb("nm_in", [B, N])
        nm = sb("nm", [N, B])
        rcnt = sb("rcnt", [N, 1])
        cnt_col = sb("cnt_col", [N, 1])
        bn6 = sb("bn6", [N, B, 6])
        var = sb("var", [N, B])
        dif = sb("dif", [N, B])
        msum = sb("msum", [N, B])
        std = sb("std", [N, B])
        rstd = sb("rstd", [N, B])
        nmr = sb("nmr", [N, B])
        adj_in = sb("adj_in", [N, 2, GS * N])
        sgn = sb("sgn", [N, GS * N], F16)
        mask = sb("mask", [N, 2, GS * N], F16)
        CH = SC * N
        work = sb("work", [N, 2 * (B * F + 4 * XC)], F16)
        y = work[:, 0:2 * B * F].bitcast(F32)
        tmp = work[:, 2 * B * F:].bitcast(F32).rearrange("p (a c) -> p a c", c=XC)
        places = [0]

        def place(size):
            places[0] += size
            assert places[0] <= 2 * (B * F + 4 * XC)
            return work[:, places[0] - size:places[0]]

        onehot = place(RING * CH)
        rs = place(2 * GS * CH).rearrange("p (u q t j) -> p u q t j", u=2, q=GS, t=SC)
        rs2 = place(2 * GS * SS * N).rearrange("p (u q t j) -> p u q t j", u=2, q=GS, t=SS)
        hostT = place(4 * GS * N).bitcast(F32).rearrange("p (u j) -> p u j", u=2)
        rankT = place(GS * N)
        host = sb("host", [N, 2, GS * N], F16)
        past = sb("past", [N, GS * N], F16)
        ranks2 = sb("ranks2", [N, GS * N], F16)
        degp = sb("degp", [N, GS])
        over = sb("over", [N, GS, NC])
        over_i = sb("over_i", [N, GS, NC], I32)
        rows_i = sb("rows_i", [N, GS, NC], I32)
        rows_or = sb("rows_or", [N, GS, NC], F16)
        nfull = sb("nfull", [N, GS])
        own = sb("own", [N, GS])
        left = sb("left", [N, GS])
        left_i = sb("left_i", [N, GS], I32)
        pieces_i = sb("pieces_i", [N, GS], I32)
        pieces = sb("pieces", [N, GS], F16)
        pad = sb("pad", [N, GS])
        start = sb("start", [N, GS])
        end = sb("end", [N, GS])
        shift = sb("shift", [N, GS])
        chunks = sb("chunks", [1, B], I32)
        neg_pad = sb("neg_pad", [N, 2, GS])
        h0 = sb("h0", [N, GS * F])
        hT0 = sb("hT0", [F + 1, 2, GS * N])
        ac32 = sb("ac32", [N, 2, 2 * H])
        ac_hi = sb("ac_hi", [N, 4, 2 * H], F16)
        ac_lo = sb("ac_lo", [N, 4, 2 * H], F16)
        acc = sb("acc", [N, 4, 4 * H])
        acc2 = sb("acc2", [N, 4 * H])
        hm = sb("hm", [N, 2, H])
        hm2 = sb("hm2", [N, 2, H])
        hmTa = sb("hmTa", [N, 2, N])
        hmTb = sb("hmTb", [H - N + 1, 2, GS * N])
        hn = sb("hn", [N, 2, (GS + 1) * F])
        hT = hT0
        msg = adj_in
        hid = acc[:, 0:2, 0:GS * N]
        upd = acc[:, 2:4, 0:GS * F]
        ss = sb("ss", [N, B])
        stat = acc2[:, 0:6 * F].rearrange("p (k f) -> p k f", f=F)

        bank = [ctx.enter_context(nc.psum_tensor(f"bank{n}", [N, 512], F32)) for n in range(8)]

        adj_v = a["adj"].rearrange("b i j -> i b j")
        x_v = a["x"].rearrange("b n f -> n b f")
        out_v = out.rearrange("b n f -> n b f")
        x3 = x[:, :].rearrange("p (b f) -> p b f", f=F)
        ds = bass.ds

        s_w0 = sem("layer0_weights_loaded")
        s_w = sem("later_weights_loaded")
        s_x = [sem(f"x_loaded{n}") for n in range(4)]
        s_adj = [sem(f"adj_loaded{p}") for p in range(2)]
        s_const = sem("constants_made")
        s_pstep = sem("pool_setup_step")
        s_vstep = sem("vector_setup_step")
        s_wmax = sem("weight_max_ready")
        s_wall = sem("weight_max_spread")
        s_nmT = sem("nodemask_transposed")
        s_nm = sem("nodemask_copied")
        s_cnt = sem("nodemask_counted")
        s_bn = sem("layernorm_stats_made")
        s_lnstep = sem("layernorm_step")
        s_var64 = sem("variances_ready")
        s_std = sem("std_ready")
        s_rstd = sem("rstd_ready")
        s_ln = sem("layernorm_scales_ready")

        def row(ap, n):
            return ap.rearrange("(a n) -> a n", a=1)

        def spread(ap, n):
            return ap.unsqueeze(0).broadcast_to([N, n])

        loads0 = [
            (w1a[:, :], a["L0_gnn_W1"][0:F, :]), (w1b[:, :], a["L0_gnn_W1"][F:2 * F, :]),
            (wac[F:F + 1, 0:H], row(a["L0_gnn_b1"], H)),
            (w2a[:, :], a["L0_gnn_W2"][0:N, :]), (w2b[0:H - N, :], a["L0_gnn_W2"][N:H, :]),
            (w2b[H - N:H - N + 1, :], row(a["L0_gnn_b2"], F)),
            (nm_in[:, :], a["nodemask"]),
        ]
        loads = [
            (l1w0[0:F, :], a["L1_gnn_W0"]), (l1w0[F:F + 1, :], row(a["L1_gnn_b0"], D1)),
            (l1w1[:, :], a["L1_gnn_W1"]), (l1w2[:, :], a["L1_gnn_W2"]), (l1wo[:, :], a["L1_gnn_Wout"]),
            (l1b1[:, :], spread(a["L1_gnn_b1"], D1)), (l1b2[:, :], spread(a["L1_gnn_b2"], D1)),
            (l1bo[:, :], spread(a["L1_gnn_bout"], F)),
            (l2w[0:F, :], a["L2_gnn_weight"]), (l2w[F:F + 1, :], row(a["L2_gnn_bias"], F)),
            (gamma[:, :], spread(a["L2_gnn_gamma"], F)), (beta[:, :], spread(a["L2_gnn_beta"], F)),
            (l3w1[:, :], a["L3_gnn_W1"]), (l3b1[:, :], a["L3_gnn_b1"].rearrange("(n a) -> n a", a=1)),
            (l3w2[0:F, :], a["L3_gnn_W2"]), (l3w2[F:F + 1, :], row(a["L3_gnn_b2"], F)),
        ]
        ALL_W0 = 16 * len(loads0)
        ALL_W = 16 * len(loads)

        def load_adj(eng, g, p):
            eng.dma_start(adj_in[:, p, :].rearrange("i (b j) -> i b j", j=N), adj_v[:, ds(GS * g, GS), :])\
               .then_inc(s_adj[p], 16)

        def layernorm_std(act, n):
            act.wait_ge(s_var64, n)
            nc.scalar.activation(std[:, :], var[:, :], ACT.Sqrt, bias=eps_col[:, 0:1], scale=1.0 / F)\
              .then_inc(s_std, 1)

        def layernorm_scales(dve, n):
            v = nc.vector
            m0, q0, m1, q1 = (bn6[:, :, k] for k in (1, 2, 4, 5))
            v.tensor_tensor(msum[:, :], m0, m1, ALU.add)
            v.tensor_tensor(dif[:, :], m0, m1, ALU.subtract)
            v.tensor_tensor(var[:, :], q0, q1, ALU.add).then_inc(s_lnstep, 1)
            dve.wait_ge(s_lnstep, 2 * n - 1)
            v.scalar_tensor_tensor(out=dif[:, :], in0=dif[:, :], scalar=F / 4.0, in1=dif[:, :],
                                   op0=ALU.mult, op1=ALU.mult).then_inc(s_lnstep, 1)
            dve.wait_ge(s_lnstep, 2 * n)
            v.tensor_tensor(var[:, :], var[:, :], dif[:, :], ALU.add).then_inc(s_var64, 1)
            dve.wait_ge(s_std, n)
            v.reciprocal(rstd[:, :], std[:, :]).then_inc(s_rstd, 1)
            dve.wait_ge(s_rstd, n)
            v.scalar_tensor_tensor(out=nmr[:, :], in0=msum[:, :], scalar=-0.5, in1=rstd[:, :],
                                   op0=ALU.mult, op1=ALU.mult).then_inc(s_ln, 1)

        def stats(b):
            return nc.vector.bn_stats(bn6[:, ds(b, 1), :].rearrange("p a t -> p (a t)"), x[:, ds(b * F, F)])

        with nc.Block() as block:
            @block.sync
            def _(sp):
                load_adj(sp, 0, 0)
                for n in range(4):
                    sp.dma_start(x3[:, 32 * n:32 * n + 32, :], x_v[:, 32 * n:32 * n + 32, :]).then_inc(s_x[n], 16)
                load_adj(sp, 1, 1)
                for dst, src in loads:
                    sp.dma_start(dst, src).then_inc(s_w, 16)

            @block.gpsimd
            def _(pool):
                g = nc.gpsimd
                g.memset(ident[:, :], 0.0)
                g.memset(ident16[:, :], 0.0)
                g.memset(before16[:, :], 1.0)
                g.memset(rankw[:, :], 1.0).then_inc(s_pstep, 1)
                pool.wait_ge(s_pstep, 1)
                for m in (ident, ident16):
                    g.affine_select(out=m[:, :], in_=m[:, :], compare_op=ALU.not_equal, fill=1.0,
                                    base=0, pattern=[[-1, N]], channel_multiplier=1)
                g.affine_select(out=before16[:, :], in_=before16[:, :], compare_op=ALU.is_gt, fill=0.0,
                                base=0, pattern=[[1, N]], channel_multiplier=-1)
                g.affine_select(out=rankw[:, :], in_=rankw[:, :], compare_op=ALU.is_ge, fill=0.0,
                                base=0, pattern=[[1, N]], channel_multiplier=-1).then_inc(s_pstep, 1)
                pool.wait_ge(s_pstep, 2)
                g.affine_select(out=rankw[:, :], in_=rankw[:, :], compare_op=ALU.not_equal, fill=KEY,
                                base=0, pattern=[[-1, N]], channel_multiplier=1)
                g.memset(ones16[:, :], 1.0)
                g.memset(ones[:, :], 1.0)
                g.memset(eps_col[:, :], EPS)
                g.memset(hn[:, :, 0:F], 0.0)
                g.iota(row_i[:, :], pattern=[[1, N]], base=0, channel_multiplier=0)
                g.iota(cand_i[:, :], pattern=[[1, NC]], base=MINC, channel_multiplier=0)
                g.iota(key_i[:, :], pattern=[[SC, MAXC + 1]], base=int(KEY), channel_multiplier=0)\
                 .then_inc(s_const, 1)
                pool.wait_ge(s_wmax, 1)
                g.partition_all_reduce(wmax_all[:, :], wmax[:, :], N, bass.bass_isa.ReduceOp.max)\
                 .then_inc(s_wall, 1)

            @block.scalar
            def _(act):
                for dst, src in loads0:
                    act.dma_start(dst, src).then_inc(s_w0, 16)
                act.wait_ge(s_const, 1)
                layernorm_std(act, 1)

            @block.tensor
            def _(pe):
                pe.wait_ge(s_const, 1)
                pe.wait_ge(s_w0, ALL_W0)
                nc.tensor.transpose(bank[0][:, 0:N], nm_in[:, :], ident[:, :]).then_inc(s_nmT, 1)
                pe.wait_ge(s_nm, 1)
                nc.tensor.matmul(bank[1][:, 0:B], ones[:, :], nm[:, :], start=True, stop=True).then_inc(s_cnt, 1)

            @block.vector
            def _(dve):
                v = nc.vector
                steps = [0]

                def settled(ins):
                    steps[0] += 1
                    ins.then_inc(s_vstep, 1)
                    dve.wait_ge(s_vstep, steps[0])

                v.memset(wmax[:, :], 0.0)
                v.memset(hT0[F:F + 1, :, :], 1.0)
                v.memset(wac[F:F + 1, H:2 * H], 0.0)

                def x_stats(n):
                    dve.wait_ge(s_x[n], 16)
                    for b in range(n * B // 4, (n + 1) * B // 4):
                        last = stats(b)
                    last.then_inc(s_bn, 1)

                x_stats(0)
                x_stats(1)
                dve.wait_ge(s_w0, ALL_W0)
                settled(v.tensor_tensor(wac[0:F, 0:H], w1a[:, :], w1b[:, :], ALU.add))
                v.tensor_copy(wac[0:F, H:2 * H], w1b[:, :])
                settled(v.tensor_scalar(wac[:, 0:H], wac[:, 0:H], -1.0, None, ALU.mult))
                v.tensor_reduce(wmax[0:F + 1, :], wac[:, :], AX.X, ALU.max, apply_absolute_value=True)\
                 .then_inc(s_wmax, 1)
                x_stats(2)
                dve.wait_ge(s_nmT, 1)
                v.tensor_copy(nm[:, :], bank[0][:, 0:B]).then_inc(s_nm, 1)
                dve.wait_ge(s_cnt, 1)
                settled(v.tensor_reduce(cnt_col[:, :], bank[1][:, 0:B], AX.X, ALU.add))
                v.reciprocal(rcnt[:, :], cnt_col[:, :])
                dve.wait_ge(s_wall, 1)
                settled(v.tensor_scalar(wmax_all[:, :], wmax_all[:, :], 2.0 ** -60, None, ALU.max))
                settled(v.tensor_scalar(wexp[:, :].bitcast(I32), wmax_all[:, :].bitcast(I32), 0x7F800000, None,
                                        ALU.bitwise_and))
                v.tensor_scalar(unscale[:, :], wexp[:, :], -(2.0 ** -8), None, ALU.mult)
                settled(v.reciprocal(wscale[:, :], wexp[:, :]))
                settled(v.tensor_scalar(wscale[:, :], wscale[:, :], 2.0 ** 8, None, ALU.mult))
                settled(v.tensor_scalar(wac[:, :], wac[:, :], wscale[0:F + 1, :], None, ALU.mult))
                dve.wait_ge(s_const, 1)
                v.tensor_copy(slot_key[:, :], key_i[:, :])
                v.tensor_copy(row_f[:, :], row_i[:, :])
                v.tensor_scalar(row_slots[:, :], row_i[0:1, :], -float(SS), None, ALU.mult)
                v.tensor_scalar(cand[:, :], cand_i[:, :], float(SC), None, ALU.mult)
                x_stats(3)
                dve.wait_ge(s_bn, 4)
                layernorm_scales(dve, 1)

        s_adjTp = sem("adj_transposed")
        s_sg = sem("sign_made")
        s_mask = sem("mask_made")
        s_rank = sem("ranks_made")
        s_rs = sem("ranks_copied")
        s_deg = sem("degree_row_copied")
        s_dc = sem("degree_columns_made")
        s_rows = sem("rows_per_candidate_made")
        s_sum = sem("rows_per_candidate_summed")
        s_nop = sem("slot_count_step")
        s_n = sem("slot_counts_ready")
        s_st = sem("first_host_rows_made")
        s_first = sem("first_host_rows_copied")
        s_hstep = sem("host_row_bounds_compared")
        s_host = sem("host_rows_ready")
        s_rkT = sem("transposed_ranks_made")
        s_rankT = sem("transposed_ranks_copied")
        s_hr = sem("host_ranks_made")
        s_hostT = sem("host_ranks_copied")
        s_rs2 = sem("host_slot_ranks_made")
        s_h = sem("h_normalised")
        s_hTp = sem("h_transposed")
        s_hT = sem("h_transpose_copied")
        s_AC = sem("AC_product_made")
        s_hi = sem("AC_high_part_made")
        s_lo = sem("AC_low_part_made")
        s_acc0 = sem("sum_initialised")
        s_G = sem("onehot_chunk_made")
        s_done = [sem(f"edges_in_bank{k}") for k, *_ in OWN]
        s_free = [sem(f"bank{k}_summed") for k, *_ in OWN]
        s_half = sem("neighbour_sums_paired")
        s_hm = sem("neighbour_sum_ready")
        s_T = sem("sum_transposed")
        s_hmT = sem("sum_transpose_copied")
        s_W2 = sem("layer0_update_made")
        s_x0 = sem("x_updated_layer0")
        s_bn0 = sem("layer1_stats_made")

        pT, pU, pSmall = bank[2][:, 0:2 * N], bank[7][:, 0:F], bank[7][:, F:F + GS * NC]
        pA3, pDeg, pH, pAC = bank[3], bank[4], bank[4], bank[2]

        def known(v):
            return isinstance(v, int)

        def pe_adj(pe, g, p, use):
            pe.wait_ge(s_adj[p], use * 16 + 16)
            pe.wait_ge(s_hostT, g)
            pe.wait_ge(s_h, g + 1)
            for q in range(GS):
                last = nc.tensor.transpose(pA3[:, q * N:(q + 1) * N], adj_in[:, p, q * N:(q + 1) * N], ident[:, :])
            last.then_inc(s_adjTp, 1)
            for q in range(GS):
                last = nc.tensor.transpose(pH[0:F, q * N:(q + 1) * N], h0[:, q * F:(q + 1) * F], ident[:, :])
            last.then_inc(s_hTp, 1)

        def pe_rank(pe, g, p):
            pe.wait_ge(s_mask, g + 1)
            pe.wait_ge(s_hT, g + 1)
            nc.tensor.matmul(pA3[:, :], rankw[:, :], mask[:, p, :], start=True, stop=True)
            nc.tensor.matmul(pDeg[F:F + 1, :], ones16[:, 0:1], mask[:, p, :], start=True, stop=True)\
              .then_inc(s_rank, 1)

        def pe_degrees(pe, g, p):
            pe.wait_ge(s_mask, g + 1)
            pe.wait_ge(s_host, g)
            for q in range(GS):
                last = nc.tensor.matmul(pSmall[:, q:q + 1], mask[:, p, q * N:(q + 1) * N], ones16[:, 0:1],
                                        start=True, stop=True)
            last.then_inc(s_dc, 1)

        def pe_sum_rows(pe, g):
            pe.wait_ge(s_rows, g + 1)
            nc.tensor.matmul(pSmall, ones16[:, :], rows_or[:, :, :].rearrange("p q c -> p (q c)"),
                             start=True, stop=True).then_inc(s_sum, 1)

        def pe_first_rows(pe, g):
            pe.wait_ge(s_n, g + 1)
            nc.tensor.matmul(pSmall[:, 0:GS], before16[:, :], pieces[:, :], start=True, stop=True).then_inc(s_st, 1)

        def pe_rank_nodes(pe, g, p):
            pe.wait_ge(s_rs, g + 1)
            for q in range(GS):
                last = nc.tensor.matmul(pA3[:, q * N:(q + 1) * N], mask[:, p, q * N:(q + 1) * N], rankw[:, :],
                                        start=True, stop=True)
            last.then_inc(s_rkT, 1)

        def pe_host_ranks(pe, g, p):
            pe.wait_ge(s_rankT, g + 1)
            pe.wait_ge(s_host, g + 1)
            pe.wait_ge(s_deg, g + 1)
            for q in range(GS):
                cols = slice(q * N, (q + 1) * N)
                nc.tensor.matmul(pA3[:, cols], rankT[:, cols], host[:, p, cols], start=True, stop=False)
                nc.tensor.matmul(pA3[:, cols], ones16[0:1, :], row_slots[:, :], start=False, stop=True)
                last = nc.tensor.matmul(pH[:, cols], host[:, p, cols], ident16[:, :], start=True, stop=True)
            last.then_inc(s_hr, 1)

        def pe_ac(pe, b, g, p, q):
            pe.wait_ge(s_hT, g + 1)
            pe.wait_ge(s_hi, b)
            if not (known(b) and b < 4):
                pe.wait_ge(s_hmT, b - 3)
            nc.tensor.matmul(pAC[:, 0:2 * H], hT0[:, p, q * N:(q + 1) * N], wac[:, :], start=True, stop=True)\
              .then_inc(s_AC, 1)

        def pe_transpose_sum(pe, b, g, p, q):
            pe.wait_ge(s_hm, b + 1)
            pe.wait_ge(s_hostT, g + 1)
            if not (known(b) and b + 4 > B):
                pe.wait_ge(s_hi, b + 4)
            else:
                pe.wait_ge(s_hmT, b)
            part = hostT[:, p, q * N:(q + 1) * N]
            nc.tensor.matmul(pT[:, 0:N], hm[:, q % 2, 0:N], ident[:, :], start=True, stop=False)
            nc.tensor.matmul(pT[:, 0:N], hm2[:, q % 2, 0:N], part, start=False, stop=True)
            nc.tensor.matmul(pT[0:H - N, N:2 * N], hm[:, q % 2, N:H], ident[:, :], start=True, stop=False)
            nc.tensor.matmul(pT[0:H - N, N:2 * N], hm2[:, q % 2, N:H], part, start=False, stop=True)\
              .then_inc(s_T, 1)

        def pe_update(pe, b, g, p, q):
            pe.wait_ge(s_hmT, b + 1)
            pe.wait_ge(s_deg, g + 1)
            pe.wait_ge(s_x0, b)
            if known(b) and b == 0:
                pe.wait_ge(s_n, 2)
            nc.tensor.matmul(pU, hmTa[:, q % 2, :], w2a[:, :], start=True, stop=False)
            nc.tensor.matmul(pU, hmTb[:, p, q * N:(q + 1) * N], w2b[:, :], start=False, stop=True).then_inc(s_W2, 1)

        def ring_place(eng, pos, chunk):
            eng.reg_alu(pos, chunk, RING - 1, ALU.bitwise_and)
            eng.reg_mul(pos, pos, CH)
            return eng.snap(pos, min_val=0, max_val=(RING - 1) * CH)

        def pe_chunk(pe, q, banks, node, regs):
            cnt, prev, full_prev, pos = regs
            pe.reg_mov(prev, cnt)
            pe.reg_add(cnt, cnt, 1)
            at = ring_place(pe, pos, prev)
            for k, n_bank, first, slots in banks:
                ps = bank[n_bank]
                pe.wait_ge(s_free[k], full_prev if k == 2 else prev)
                for e, part in enumerate((ac_hi, ac_lo)):
                    nc.tensor.matmul(ps[:, 0:slots * H].rearrange("p (t h) -> p t h", t=slots), node,
                                     part[:, q, 0:H].unsqueeze(1).broadcast_to([N, slots, H]),
                                     start=(e == 0), stop=False)
                if k == 0:
                    pe.wait_ge(s_G, cnt)
                for t in range(slots):
                    hot = onehot[:, ds(at + (first + t) * N, N)]
                    for e, part in enumerate((ac_hi, ac_lo)):
                        last = nc.tensor.matmul(ps[:, t * H:(t + 1) * H], hot, part[:, q, H:2 * H],
                                                start=False, stop=(e == 1 and t == slots - 1))
                last.then_inc(s_done[k], 1)

        def pe_slots(pe, b, g, u, q, regs, between):
            pe.wait_ge(s_lo, b + 1)
            pe.wait_ge(s_n, g + 1)
            n = pe.value_load(chunks[0:1, ds(b, 1)], min_val=MINC + 1, max_val=MAXC)
            with pe.Fori(0, n - 1):
                pe_chunk(pe, q, OWN, ident16[:, :], regs)
                pe.reg_add(regs[2], regs[2], 1)
            between()
            pe.wait_ge(s_host, g + 1)
            pe_chunk(pe, q, SHARED, host[:, u, q * N:(q + 1) * N], regs)

        def around(i, body, *more):
            for u in range(2):
                g = 2 * i + u
                for q in range(GS):
                    nxt = None if known(g) and g == NG - 1 else g + 1
                    body(8 * i + 4 * u + q, g, u, q, nxt, 1 - u, i if u == 0 else i + 1)

        def all_iterations(eng, body):
            around(0, body)
            with eng.Fori(1, NI - 1) as i:
                around(i, body)
            around(NI - 1, body)

        def group_of(b, g, u, q, back):
            r = q - back
            if 0 <= r < GS:
                return g, u, r
            return (g - 1, 1 - u, r + GS) if r < 0 else (g + 1, 1 - u, r - GS)

        def act_adj(act, g, p):
            act.wait_ge(s_adjTp, g + 1)
            nc.scalar.activation(adjT[:, ds(g * (GS * N), GS * N)], pA3[:, :], ACT.Copy)
            nc.scalar.activation(sgn[:, :], pA3[:, :], ACT.Sign).then_inc(s_sg, 1)
            act.wait_ge(s_sg, g + 1)
            nc.scalar.activation(mask[:, p, :], sgn[:, :], ACT.Relu).then_inc(s_mask, 1)
            act.wait_ge(s_hTp, g + 1)
            nc.scalar.activation(hT0[0:F, p, :], pH[0:F, :], ACT.Copy).then_inc(s_hT, 1)

        def act_h(act, g):
            act.wait_ge(s_hTp, g)
            for q in range(GS):
                last = nc.scalar.activation(h0[:, q * F:(q + 1) * F], x[:, ds((g * GS + q) * F, F)], ACT.Relu,
                                            bias=nmr[:, ds(g * GS + q, 1)], scale=rstd[:, ds(g * GS + q, 1)])
            last.then_inc(s_h, 1)

        def act_rank(act, g, p):
            act.wait_ge(s_rank, g + 1)
            for t in range(SC):
                last = nc.scalar.activation(rs[:, p, :, t, :], pA3[:, :].rearrange("p (q j) -> p q j", q=GS),
                                            ACT.Copy, bias=-float(t))
            last.then_inc(s_rs, 1)

        def act_rank_nodes(act, g):
            act.wait_ge(s_rkT, g + 1)
            act.wait_ge(s_first, g + 1)
            for q in range(GS):
                cols = slice(q * N, (q + 1) * N)
                last = nc.scalar.activation(rankT[:, cols], pA3[:, cols], ACT.Identity, bias=shift[:, q:q + 1])
            last.then_inc(s_rankT, 1)

        def act_host_ranks(act, g, p):
            act.wait_ge(s_hr, g + 1)
            nc.scalar.activation(ranks2[:, :], pA3[:, :], ACT.Copy)
            nc.scalar.activation(hostT[:, p, :], pH[:, :], ACT.Copy).then_inc(s_hostT, 1)
            act.wait_ge(s_hostT, g + 1)
            for t in range(SS):
                last = nc.scalar.activation(rs2[:, p, :, t, :], ranks2[:, :].rearrange("p (q j) -> p q j", q=GS),
                                            ACT.Copy, bias=-float(t))
            last.then_inc(s_rs2, 1)

        def act_degrees(act, g, p, updates):
            act.wait_ge(s_rank, g + 1)
            if updates is not None:
                act.wait_ge(s_W2, updates)
            nc.scalar.activation(hmTb[F:F + 1, p, :], pDeg[F:F + 1, :], ACT.Copy).then_inc(s_deg, 1)

        def act_ac(act, b, q):
            act.wait_ge(s_AC, b + 1)
            if not (known(b) and b < 2):
                act.wait_ge(s_lo, b - 1)
                act.wait_ge(s_acc0, b - 1)
            nc.scalar.activation(ac32[:, q % 2, :], pAC[:, 0:2 * H], ACT.Copy)
            nc.scalar.activation(ac_hi[:, q, :], pAC[:, 0:2 * H], ACT.Copy).then_inc(s_hi, 1)

        def act_init(act, b, g, p, q):
            act.wait_ge(s_n, g + 1)
            act.wait_ge(s_hi, b + 1)
            if not (known(b) and b < 4):
                act.wait_ge(s_hm, b - 3)
            nc.scalar.activation(acc[:, q, :].rearrange("p (t h) -> p t h", t=4),
                                 ac32[:, q % 2, 0:H].unsqueeze(1).broadcast_to([N, 4, H]), ACT.Relu,
                                 scale=neg_pad[:, p, q:q + 1]).then_inc(s_acc0, 1)

        def act_sum(act, b, p, q):
            act.wait_ge(s_T, b + 1)
            nc.scalar.activation(hmTa[:, q % 2, :], pT[:, 0:N], ACT.Copy, scale=unscale[:, 0:1])
            nc.scalar.activation(hmTb[0:H - N, p, q * N:(q + 1) * N], pT[0:H - N, N:2 * N], ACT.Copy,
                                 scale=unscale[0:H - N, 0:1]).then_inc(s_hmT, 1)

        def dve_rows(dve, g):
            v = nc.vector
            dve.wait_ge(s_dc, g + 1)
            v.tensor_scalar(degp[:, :], pSmall[:, 0:GS], float(SS - 1), None, ALU.add).then_inc(s_nop, 1)
            dve.wait_ge(s_nop, 12 * g + 1)
            v.tensor_tensor(over[:, :, :], degp[:, :].unsqueeze(2).broadcast_to([N, GS, NC]),
                            cand[:, :].unsqueeze(1).broadcast_to([N, GS, NC]), ALU.subtract).then_inc(s_nop, 1)
            dve.wait_ge(s_nop, 12 * g + 2)
            v.tensor_scalar(over_i[:, :, :], over[:, :, :], float(SS - 1), float(DIV), ALU.max, ALU.mult)\
             .then_inc(s_nop, 1)
            dve.wait_ge(s_nop, 12 * g + 3)
            v.tensor_scalar(rows_i[:, :, :], over_i[:, :, :], SH, None, ALU.arith_shift_right).then_inc(s_nop, 1)
            dve.wait_ge(s_nop, 12 * g + 4)
            v.tensor_copy(rows_or[:, :, :], rows_i[:, :, :]).then_inc(s_rows, 1)

        def dve_counts(dve, g, p):
            v = nc.vector
            dve.wait_ge(s_sum, g + 1)
            v.tensor_scalar(over[:, :, :], pSmall.rearrange("p (q c) -> p q c", q=GS), float(N), None, ALU.is_gt)\
             .then_inc(s_nop, 1)
            dve.wait_ge(s_nop, 12 * g + 5)
            v.tensor_reduce(nfull[:, :], over[:, :, :], AX.X, ALU.add).then_inc(s_nop, 1)
            dve.wait_ge(s_nop, 12 * g + 6)
            v.tensor_scalar(chunks[:, ds(g * GS, GS)], nfull[0:1, :], float(MINC + 1), None, ALU.add)
            v.tensor_scalar(own[:, :], nfull[:, :], float(SC), float(SC * MINC), ALU.mult, ALU.add).then_inc(s_nop, 1)
            dve.wait_ge(s_nop, 12 * g + 7)
            v.tensor_tensor(left[:, :], degp[:, :], own[:, :], ALU.subtract).then_inc(s_nop, 1)
            dve.wait_ge(s_nop, 12 * g + 8)
            v.tensor_scalar(left_i[:, :], left[:, :], float(SS - 1), float(DIV), ALU.max, ALU.mult).then_inc(s_nop, 1)
            dve.wait_ge(s_nop, 12 * g + 9)
            v.tensor_scalar(pieces_i[:, :], left_i[:, :], SH, None, ALU.arith_shift_right).then_inc(s_nop, 1)
            dve.wait_ge(s_nop, 12 * g + 10)
            v.tensor_copy(pieces[:, :], pieces_i[:, :])
            v.scalar_tensor_tensor(out=pad[:, :], in0=pieces_i[:, :], scalar=-float(SS), in1=left[:, :],
                                   op0=ALU.mult, op1=ALU.add).then_inc(s_nop, 1)
            dve.wait_ge(s_nop, 12 * g + 11)
            v.tensor_scalar(neg_pad[:, p, :], pad[:, :], -float(SS - 1), 0.25, ALU.add, ALU.mult).then_inc(s_n, 1)

        def dve_first_rows(dve, g):
            dve.wait_ge(s_st, g + 1)
            dve.wait_ge(s_host, g)
            nc.vector.tensor_copy(start[:, :], pSmall[:, 0:GS])
            nc.vector.tensor_tensor(end[:, :], pSmall[:, 0:GS], pieces[:, :], ALU.add)
            nc.vector.scalar_tensor_tensor(out=shift[:, :], in0=pSmall[:, 0:GS], scalar=float(SS), in1=own[:, :],
                                           op0=ALU.mult, op1=ALU.subtract).then_inc(s_first, 1)
            dve.wait_ge(s_first, g + 1)
            for q in range(GS):
                last = nc.vector.tensor_scalar(past[:, q * N:(q + 1) * N], row_f[:, :], end[:, q:q + 1], None, ALU.is_ge)
            last.then_inc(s_nop, 1)

        def dve_onehot(ranks, slots, key, at):
            nc.vector.tensor_scalar(onehot[:, ds(at, slots * N)], ranks.rearrange("p t j -> p (t j)"),
                                    slot_key[:, ds(key, 1)], None, ALU.is_equal).then_inc(s_G, 1)

        def dve_slots(dve, b, g, u, q, regs, between):
            cnt, prev, full, full_prev, pos, count_reg = regs
            n = dve.snap(count_reg, min_val=MINC + 1, max_val=MAXC)

            def count():
                dve.reg_mov(prev, cnt)
                dve.reg_add(cnt, cnt, 1)
                return ring_place(dve, pos, cnt)

            def own_chunk():
                dve.reg_mov(full_prev, full)
                dve.reg_add(full, full, 1)
                for k, n_bank, _, slots in OWN:
                    sums = acc[:, q, (k % 2) * 2 * H:(k % 2) * 2 * H + slots * H]
                    dve.wait_ge(s_done[k], full if k == 2 else cnt)
                    if k == 0:
                        dve.wait_ge(s_free[2], full_prev)
                    elif k == 1:
                        dve.wait_ge(s_free[3], prev)
                    else:
                        dve.wait_ge(s_free[k - 2], cnt)
                    nc.vector.scalar_tensor_tensor(out=sums, in0=bank[n_bank][:, 0:slots * H], scalar=0.0, in1=sums,
                                                   op0=ALU.min, op1=ALU.add).then_inc(s_free[k], 1)

            def shared_chunk():
                for k, n_bank, _, slots in SHARED:
                    sums = acc2[:, (k % 2) * 2 * H:(k % 2) * 2 * H + slots * H]
                    ps = bank[n_bank][:, 0:slots * H]
                    dve.wait_ge(s_done[k], cnt)
                    if k < 2:
                        nc.vector.tensor_scalar(sums, ps, 0.0, None, ALU.min).then_inc(s_free[k], 1)
                    else:
                        dve.wait_ge(s_free[k - 2], cnt)
                        nc.vector.scalar_tensor_tensor(out=sums, in0=ps, scalar=0.0, in1=sums,
                                                       op0=ALU.min, op1=ALU.add).then_inc(s_free[k], 1)

            with dve.Fori(0, n - 2) as c:
                dve_onehot(rs[:, u, q, :, :], SC, c + 1, count())
                own_chunk()
            at = count()
            dve.wait_ge(s_rs2, g + 1)
            dve_onehot(rs2[:, u, q, :, :], SS, 0, at)
            own_chunk()
            at = count()
            if not (known(b) and b == B - 1):
                g1, p1, q1 = group_of(b, g, u, q, -1)
                dve.wait_ge(s_rs, g1 + 1)
                dve_onehot(rs[:, p1, q1, :, :], SC, 0, at)
                dve.wait_ge(s_acc0, b + 2)
                dve.wait_ge(s_n, g1 + 1)
                dve.reg_load(count_reg, chunks[0:1, ds(b + 1, 1)])
            between()
            dve.wait_ge(s_hm, b)
            shared_chunk()

        def dve_update(dve, b):
            xb = x[:, ds(b * F, F)]
            dve.wait_ge(s_x0, b)
            dve.wait_ge(s_W2, b + 1)
            nc.vector.tensor_tensor(xb, pU, xb, ALU.add).then_inc(s_x0, 1)
            if not (known(b) and b == 0):
                stats(b - 1)

        def pool_low(pool, b, q):
            pool.wait_ge(s_hi, b + 1)
            nc.gpsimd.tensor_tensor(ac_lo[:, q, :], ac32[:, q % 2, :], ac_hi[:, q, :], ALU.subtract)\
              .then_inc(s_lo, 1)

        def pool_hosts(pool, g, p, turn):
            pool.wait_ge(s_first, g + 1 if known(g) else turn)
            pool.reg_add(turn, turn, 1)
            for q in range(GS):
                last = nc.gpsimd.tensor_scalar(host[:, p, q * N:(q + 1) * N], row_f[:, :], start[:, q:q + 1], None,
                                               ALU.is_ge)
            last.then_inc(s_hstep, 1)
            pool.wait_ge(s_nop, 12 * g + 12)
            pool.wait_ge(s_hstep, g + 1)
            nc.gpsimd.tensor_tensor(host[:, p, :], host[:, p, :], past[:, :], ALU.subtract).then_inc(s_host, 1)

        def pool_sum(pool, b, g, q, total):
            pool.wait_ge(s_n, g + 1)
            n = pool.value_load(chunks[0:1, ds(b, 1)], min_val=MINC + 1, max_val=MAXC)
            pool.reg_add(total, total, n)
            for k, *_ in SHARED:
                pool.wait_ge(s_free[k], total)
            for t in (acc[:, q, :], acc2[:, :]):
                last = nc.gpsimd.tensor_tensor(t[:, 0:2 * H], t[:, 0:2 * H], t[:, 2 * H:4 * H], ALU.add)
            last.then_inc(s_half, 1)
            pool.wait_ge(s_half, b + 1)
            nc.gpsimd.tensor_tensor(hm[:, q % 2, :], acc[:, q, 0:H], acc[:, q, H:2 * H], ALU.add)
            nc.gpsimd.tensor_tensor(hm2[:, q % 2, :], acc2[:, 0:H], acc2[:, H:2 * H], ALU.add).then_inc(s_hm, 1)

        with nc.Block() as block:
            @block.sync
            def _(sp):
                with sp.Fori(1, NI) as i:
                    for p in range(2):
                        sp.wait_ge(s_adjTp, 2 * i + p - 1)
                        load_adj(sp, 2 * i + p, p)

            @block.tensor
            def _(pe):
                regs = [pe.alloc_register(f"pe_{r}") for r in ("chunk", "chunk_before", "own_before", "ring_place")]
                pe.reg_mov(regs[0], 0)
                pe.reg_mov(regs[2], 0)
                pe_adj(pe, 0, 0, 0)
                pe_rank(pe, 0, 0)
                pe_degrees(pe, 0, 0)
                pe_ac(pe, 0, 0, 0, 0)
                pe_sum_rows(pe, 0)
                pe_ac(pe, 1, 0, 0, 1)
                pe_first_rows(pe, 0)
                pe_rank_nodes(pe, 0, 0)
                pe_host_ranks(pe, 0, 0)

                def step(b, g, u, q, nxt, p, use):
                    if nxt is not None:
                        if q == 0:
                            pe_adj(pe, nxt, p, use)
                        if q == 3:
                            pe_rank_nodes(pe, nxt, p)
                    if not (known(b) and b + 2 >= B):
                        pe_ac(pe, b + 2, *group_of(b, g, u, q, -2))

                    def between():
                        if not (known(b) and b < 1):
                            pe_transpose_sum(pe, b - 1, *group_of(b, g, u, q, 1))
                        if not (known(b) and b < 2):
                            pe_update(pe, b - 2, *group_of(b, g, u, q, 2))
                        if nxt is not None:
                            if q == 0:
                                pe_rank(pe, nxt, p)
                                pe_degrees(pe, nxt, p)
                            if q == 1:
                                pe_sum_rows(pe, nxt)
                            if q == 2:
                                pe_first_rows(pe, nxt)
                            if q == 3:
                                pe_host_ranks(pe, nxt, p)

                    pe_slots(pe, b, g, u, q, regs, between)

                all_iterations(pe, step)
                pe_transpose_sum(pe, B - 1, NG - 1, 1, 3)
                pe_update(pe, B - 2, NG - 1, 1, 2)
                pe_update(pe, B - 1, NG - 1, 1, 3)

            @block.scalar
            def _(act):
                act_h(act, 0)
                act_adj(act, 0, 0)
                act_h(act, 1)
                act_rank(act, 0, 0)
                act_degrees(act, 0, 0, None)
                act_ac(act, 0, 0)
                act_ac(act, 1, 1)
                act_init(act, 0, 0, 0, 0)
                act_rank_nodes(act, 0)
                act_host_ranks(act, 0, 0)

                def step(b, g, u, q, nxt, p, use):
                    if nxt is not None:
                        if q == 0:
                            act_adj(act, nxt, p)
                        if q == 1:
                            act_rank(act, nxt, p)
                        if q == 2:
                            act_degrees(act, nxt, p, None if known(nxt) and nxt < 2 else GS * nxt - GS)
                    if not (known(b) and b + 2 >= B):
                        act_ac(act, b + 2, (q + 2) % GS)
                    if not (known(b) and b + 1 >= B):
                        act_init(act, b + 1, *group_of(b, g, u, q, -1))
                    if q == 1 and not (known(g) and g + 2 >= NG):
                        act_h(act, g + 2)
                    if nxt is not None and q == 3:
                        act_rank_nodes(act, nxt)
                    if not (known(b) and b < 1):
                        act_sum(act, b - 1, *group_of(b, g, u, q, 1)[1:])
                    if nxt is not None and q == 3:
                        act_host_ranks(act, nxt, p)

                all_iterations(act, step)
                act_sum(act, B - 1, 1, 3)

            @block.vector
            def _(dve):
                regs = [dve.alloc_register(f"dve_{r}")
                        for r in ("chunk", "chunk_before", "own", "own_before", "ring_place", "slot_chunks")]
                dve.reg_mov(regs[0], 0)
                dve.reg_mov(regs[2], 0)
                dve_rows(dve, 0)
                dve_counts(dve, 0, 0)
                dve_first_rows(dve, 0)
                dve.wait_ge(s_rs, 1)
                dve_onehot(rs[:, 0, 0, :, :], SC, 0, 0)
                dve.wait_ge(s_acc0, 1)
                dve.wait_ge(s_n, 1)
                dve.reg_load(regs[5], chunks[0:1, 0:1])

                def step(b, g, u, q, nxt, p, use):
                    def between():
                        if nxt is not None:
                            if q == 0:
                                dve_rows(dve, nxt)
                            if q == 1:
                                dve_counts(dve, nxt, p)
                            if q == 2:
                                dve_first_rows(dve, nxt)
                        if not (known(b) and b < 2):
                            dve_update(dve, b - 2)

                    dve_slots(dve, b, g, u, q, regs, between)

                all_iterations(dve, step)
                for b in range(B - 2, B):
                    dve_update(dve, b)
                dve.wait_ge(s_x0, B)
                stats(B - 1).then_inc(s_bn0, 1)

            @block.gpsimd
            def _(pool):
                total = pool.alloc_register("pool_chunks")
                pool.reg_mov(total, 0)
                pool_low(pool, 0, 0)
                pool_low(pool, 1, 1)
                turn = pool.alloc_register("pool_hosts_turn")
                pool.reg_mov(turn, 1)
                pool_hosts(pool, 0, 0, turn)

                def step(b, g, u, q, nxt, p, use):
                    if not (known(b) and b + 2 >= B):
                        pool_low(pool, b + 2, (q + 2) % GS)
                    if nxt is not None and q == 2:
                        pool_hosts(pool, nxt, p, turn)
                    pool_sum(pool, b, g, q, total)

                all_iterations(pool, step)

        s_hn1 = [sem(f"l1_h_normalised{u}") for u in range(2)]
        s_p1 = [sem(f"l1_stage_done{u}") for u in range(2)]
        s_c1 = [sem(f"l1_stage_copied{u}") for u in range(2)]
        s_t1 = [sem(f"l1_update_step{u}") for u in range(2)]
        s_bn1 = sem("layer2_stats_made")
        ST = 7
        s_one = sem("l1_ones_set")
        h1 = work[:, 0:4 * GS * (F + 1)].bitcast(F32).rearrange("p (u q f) -> p u q f", u=2, q=GS)
        aggT = work[0:F + 1, 4 * GS * (F + 1):4 * GS * (F + 1) + 4 * GS * N].bitcast(F32)\
            .rearrange("p (u j) -> p u j", u=2)

        def norm_h1(u, b, q):
            ins = nc.scalar.activation(h1[:, u, q, 0:F], x[:, ds((b + q) * F, F)], ACT.Relu,
                                       bias=nmr[:, ds(b + q, 1)], scale=rstd[:, ds(b + q, 1)])
            if q == GS - 1:
                ins.then_inc(s_hn1[u], 1)

        def l1_bank(u, st):
            return bank[4 * u + (2 if st == ST - 1 else st % 2)]

        def norm_graph(s_done, u, b, q, last):
            ins = nc.scalar.activation(hn[:, u, (q + 1) * F:(q + 2) * F], x[:, ds((b + q) * F, F)], ACT.Relu,
                                       bias=nmr[:, ds(b + q, 1)], scale=rstd[:, ds(b + q, 1)])
            if last:
                ins.then_inc(s_done, 1)

        def grp(u, i):
            return 2 * i + u

        with nc.Block() as block:
            @block.tensor
            def _(pe):
                turn = [pe.alloc_register(f"l1_turn{u}") for u in range(2)]
                for u in range(2):
                    pe.reg_mov(turn[u], 1)
                pe.wait_ge(s_w, ALL_W)
                pe.wait_ge(s_one, 1)
                with pe.Fori(0, NI) as i:
                    for st in range(ST):
                        for u in range(2):
                            ps = l1_bank(u, st)
                            b0 = GS * grp(u, i)
                            pe.wait_ge(s_c1[u], ST * i + st)
                            if st == 0:
                                pe.wait_ge(s_hn1[u], turn[u])
                                pe.reg_add(turn[u], turn[u], 1)
                            if st == 1:
                                last = nc.tensor.matmul(ps[:, :], l1w0[:, :], aggT[:, u, :], start=True, stop=True)
                            for q in range(GS if st != 1 else 0):
                                cols = slice(q * N, (q + 1) * N)
                                if st == 0:
                                    last = nc.tensor.matmul(ps[0:F + 1, cols], h1[:, u, q, :],
                                                            adjT[:, ds((b0 + q) * N, N)], start=True, stop=True)
                                elif st in (3, 5):
                                    last = nc.tensor.matmul(ps[:, cols], msg[:, u, cols],
                                                            adjT[:, ds((b0 + q) * N, N)], start=True, stop=True)
                                elif st in (2, 4):
                                    w = l1w1 if st == 2 else l1w2
                                    last = nc.tensor.matmul(ps[:, cols], hid[:, u, cols], w[:, :], start=True, stop=True)
                                else:
                                    last = nc.tensor.matmul(ps[:, q * F:(q + 1) * F], hid[:, u, cols], l1wo[:, :],
                                                            start=True, stop=True)
                            last.then_inc(s_p1[u], 1)

            @block.scalar
            def _(act):
                layernorm_std(act, 2)
                act.wait_ge(s_ln, 2)
                for u in range(2):
                    for q in range(GS):
                        norm_h1(u, GS * u, q)

                def group_pair(i, more):
                    for st in range(ST):
                        for u in range(2):
                            ps = l1_bank(u, st)
                            if st in (0, 1, 3, 5):
                                act.wait_ge(s_p1[u], ST * i + st + 1)
                            if st == 0:
                                nc.scalar.activation(aggT[:, u, :], ps[0:F + 1, :], ACT.Copy).then_inc(s_c1[u], 1)
                            elif st in (1, 3, 5):
                                nc.scalar.activation(hid[:, u, :], ps[:, :], ACT.Relu).then_inc(s_c1[u], 1)
                            elif more:
                                for q in {2: (0,), 4: (1,), 6: (2, 3)}[st]:
                                    norm_h1(u, GS * grp(u, i + 1), q)

                with act.Fori(0, NI - 1) as i:
                    group_pair(i, True)
                group_pair(NI - 1, False)

            @block.gpsimd
            def _(pool):
                nc.gpsimd.memset(h1[:, :, :, F:F + 1], 1.0).then_inc(s_one, 1)

            @block.vector
            def _(dve):
                dve.wait_ge(s_bn0, 1)
                layernorm_scales(dve, 2)

                dve.wait_ge(s_w, ALL_W)

                def pair_stats(i, first, count):
                    for e in range(first, first + count):
                        last = stats(2 * GS * i + e)
                    return last

                def group_pair(i, before):
                    for st in (2, 4):
                        for u in range(2):
                            dve.wait_ge(s_p1[u], ST * i + st + 1)
                            bias = l1b1 if st == 2 else l1b2
                            nc.vector.tensor_tensor(
                                msg[:, u, :].rearrange("p (q d) -> p q d", q=GS),
                                l1_bank(u, st)[:, :].rearrange("p (q d) -> p q d", q=GS),
                                bias[:, :].unsqueeze(1).broadcast_to([N, GS, D1]), ALU.add).then_inc(s_c1[u], 1)
                        if before is not None:
                            if st == 2:
                                for u in range(2):
                                    dve.wait_ge(s_t1[u], 2 * i)
                            last = pair_stats(before, 0 if st == 2 else GS, GS)
                            if st == 4:
                                last.then_inc(s_bn1, 1)
                    up3 = [upd[:, u, :].rearrange("p (q f) -> p q f", q=GS) for u in range(2)]
                    for u in range(2):
                        dve.wait_ge(s_p1[u], ST * i + ST)
                        nc.vector.tensor_tensor(up3[u], l1_bank(u, ST - 1)[:, 0:GS * F].rearrange("p (q f) -> p q f", q=GS),
                                                l1bo[:, :].unsqueeze(1).broadcast_to([N, GS, F]), ALU.add)\
                          .then_inc(s_c1[u], 1)
                    for u in range(2):
                        dve.wait_ge(s_c1[u], ST * i + ST)
                        nc.vector.tensor_tensor(up3[u], up3[u],
                                                nm[:, ds(GS * grp(u, i), GS)].unsqueeze(2).broadcast_to([N, GS, F]),
                                                ALU.mult).then_inc(s_t1[u], 1)
                    for u in range(2):
                        xg = x[:, ds(GS * grp(u, i) * F, GS * F)]
                        dve.wait_ge(s_t1[u], 2 * i + 1)
                        nc.vector.tensor_tensor(xg, xg, upd[:, u, :], ALU.add).then_inc(s_t1[u], 1)

                group_pair(0, None)
                with dve.Fori(1, NI) as i:
                    group_pair(i, i - 1)
                for u in range(2):
                    dve.wait_ge(s_t1[u], 2 * NI)
                pair_stats(NI - 1, 0, 2 * GS).then_inc(s_bn1, 1)

        s_hn2 = [sem(f"l2_h_normalised{u}") for u in range(2)]
        s_p2 = [sem(f"l2_stage_done{u}") for u in range(2)]
        s_c2 = [sem(f"l2_stage_copied{u}") for u in range(2)]
        s_q2 = [sem(f"l2_squares_made{u}") for u in range(2)]
        s_n2 = [sem(f"l2_row_sums_made{u}") for u in range(2)]

        with nc.Block() as block:
            @block.tensor
            def _(pe):
                with pe.Fori(0, NI) as i:
                    for st in range(2):
                        for u in range(2):
                            ps = bank[4 * u + st]
                            b0 = GS * grp(u, i)
                            if st > 0:
                                pe.wait_ge(s_c2[u], 2 * i + st)
                            if st == 0:
                                pe.wait_ge(s_hn2[u], i + 1)
                            for q in range(GS):
                                cols = slice(q * N, (q + 1) * N)
                                if st == 0:
                                    hq = hn[:, u, (q + 1) * F:(q + 2) * F]
                                    nc.tensor.matmul(ps[0:F, cols], hq, adjT[:, ds((b0 + q) * N, N)],
                                                     start=True, stop=False)
                                    last = nc.tensor.matmul(ps[0:F, cols], hq, ident[:, :], start=False, stop=True)
                                else:
                                    last = nc.tensor.matmul(ps[:, q * F:(q + 1) * F], hT[:, u, cols], l2w[:, :],
                                                            start=True, stop=True)
                            last.then_inc(s_p2[u], 1)

            @block.scalar
            def _(act):
                layernorm_std(act, 3)
                act.wait_ge(s_ln, 3)
                for u in range(2):
                    for q in range(GS):
                        norm_graph(s_hn2[u], u, GS * u, q, q == GS - 1)

                def group_pair(i, more):
                    if more:
                        for u in range(2):
                            act.wait_ge(s_p2[u], 2 * i + 1)
                            for q in range(GS):
                                norm_graph(s_hn2[u], u, GS * grp(u, i + 1), q, q == GS - 1)
                    for u in range(2):
                        b0 = GS * grp(u, i)
                        act.wait_ge(s_p2[u], 2 * i + 2)
                        nc.scalar.activation(y[:, ds(b0 * F, GS * F)], bank[4 * u + 1][:, 0:GS * F], ACT.Copy)
                        act.wait_ge(s_n2[u], i)
                        nc.scalar.activation(upd[:, u, :], bank[4 * u + 1][:, 0:GS * F], ACT.Square)\
                          .then_inc(s_c2[u], 1)

                with act.Fori(0, NI - 1) as i:
                    group_pair(i, True)
                group_pair(NI - 1, False)

            @block.vector
            def _(dve):
                dve.wait_ge(s_bn1, NI)
                layernorm_scales(dve, 3)
                with dve.Fori(0, NI) as i:
                    for u in range(2):
                        dve.wait_ge(s_p2[u], 2 * i + 1)
                        nc.vector.tensor_copy(hT[0:F, u, :], bank[4 * u][0:F, :]).then_inc(s_c2[u], 1)
                    for u in range(2):
                        dve.wait_ge(s_c2[u], 2 * i + 2)
                        nc.vector.tensor_reduce(ss[:, ds(GS * grp(u, i), GS)],
                                                upd[:, u, :].rearrange("p (q f) -> p q f", q=GS), AX.X, ALU.add)\
                          .then_inc(s_n2[u], 1)

        s_nrm = sem("row_norms_ready")
        s_y = [sem(f"y_chunk_normalised{k}") for k in range(2)]
        s_cutmask = sem("block_mask_step")
        s_ms = sem("y_masked_sums_made")
        s_blk = sem("own_blocks_cut")
        s_tot = sem("blocks_added_up")
        s_vb = sem("batchnorm_step")
        s_mean = sem("batchnorm_mean_ready")
        s_d = [sem(f"y_chunk_centred{k}") for k in range(2)]
        s_dq = sem("y_chunk_squared")
        s_dms = sem("y_square_chunk_summed")
        s_var = sem("batchnorm_std_ready")
        s_ya = sem("y_chunk_scaled")
        s_yb = sem("y_chunk_shifted")
        s_yc = sem("y_chunk_masked_relu")
        s_xn = [sem(f"x_updated_layer2_{k}") for k in range(2)]
        s_bn2 = sem("layer3_stats_made")
        AHEAD = 3

        blk, block_mask = tmp[0:GX, 0, :], tmp[0:GX, 1, :]

        def yc(c):
            return y[:, ds(c * XC, XC)]

        def xc(c):
            return x[:, ds(c * XC, XC)]

        def g3(ap):
            return ap.rearrange("p (g f) -> p g f", f=F)

        def per_graph(t, c):
            return t[:, ds(c * GX, GX)].unsqueeze(2).broadcast_to([N, GX, F])

        def per_feature(t):
            return t.unsqueeze(1).broadcast_to([N, GX, F])

        def normalise(eng, ops, k):
            with eng.Fori(0, NXC // 2) as n:
                c = 2 * n + k
                ops.tensor_tensor(g3(yc(c)), g3(yc(c)), per_graph(ss, c), ALU.mult).then_inc(s_y[k], 1)

        def centre(eng, ops, k):
            with eng.Fori(0, NXC // 2) as n:
                c = 2 * n + k
                ops.tensor_tensor(g3(yc(c)), g3(yc(c)), per_feature(stat[:, 1, :]), ALU.subtract).then_inc(s_d[k], 1)

        with nc.Block() as block:
            @block.tensor
            def _(pe):
                for c in range(NXC):
                    pe.wait_ge(s_y[c % 2], c // 2 + 1)
                    last = nc.tensor.matmul(bank[0][0:GX, :], nm[:, c * GX:(c + 1) * GX], y[:, c * XC:(c + 1) * XC],
                                            start=(c == 0), stop=(c == NXC - 1))
                last.then_inc(s_ms, 1)
                pe.wait_ge(s_blk, 1)
                nc.tensor.matmul(bank[1][:, :], ones[0:GX, :], blk, start=True, stop=True).then_inc(s_tot, 1)
                for c in range(NXC):
                    pe.wait_ge(s_dq, c + 1)
                    nc.tensor.matmul(bank[2][0:GX, :], nm[:, c * GX:(c + 1) * GX], tmp[:, 2 + c % 2, :],
                                     start=(c == 0), stop=(c == NXC - 1)).then_inc(s_dms, 1)
                pe.wait_ge(s_blk, 2)
                nc.tensor.matmul(bank[3][:, :], ones[0:GX, :], blk, start=True, stop=True).then_inc(s_tot, 1)

            @block.vector
            def _(dve):
                v = nc.vector
                steps = [0]

                def settled(ins):
                    steps[0] += 1
                    ins.then_inc(s_vb, 1)
                    dve.wait_ge(s_vb, steps[0])

                dve.wait_ge(s_nrm, 1)
                settled(v.tensor_scalar(ss[:, :], ss[:, :], 1e-12, None, ALU.max))
                settled(v.reciprocal(ss[:, :], ss[:, :]))
                normalise(dve, v, 0)
                dve.wait_ge(s_ms, 1)
                dve.wait_ge(s_cutmask, 3)
                v.tensor_tensor(blk, bank[0][0:GX, :], block_mask, ALU.mult).then_inc(s_blk, 1)
                dve.wait_ge(s_tot, 1)
                settled(v.tensor_reduce(stat[:, 0, :], bank[1][:, :].rearrange("p (g f) -> p f g", f=F), AX.X, ALU.add))
                v.tensor_scalar(stat[:, 1, :], stat[:, 0, :], rcnt[:, :], None, ALU.mult).then_inc(s_mean, 1)
                dve.wait_ge(s_mean, 1)
                centre(dve, v, 0)
                dve.wait_ge(s_dms, NXC)
                v.tensor_tensor(blk, bank[2][0:GX, :], block_mask, ALU.mult).then_inc(s_blk, 1)
                dve.wait_ge(s_tot, 2)
                settled(v.tensor_reduce(stat[:, 2, :], bank[3][:, :].rearrange("p (g f) -> p f g", f=F), AX.X, ALU.add))
                settled(v.tensor_scalar(stat[:, 3, :], stat[:, 2, :], rcnt[:, :], None, ALU.mult))
                dve.wait_ge(s_var, 1)
                settled(v.reciprocal(stat[:, 5, :], stat[:, 4, :]))
                settled(v.tensor_tensor(stat[:, 5, :], stat[:, 5, :], gamma[:, :], ALU.mult))

                def scale(c):
                    v.tensor_tensor(g3(yc(c)), g3(yc(c)), per_feature(stat[:, 5, :]), ALU.mult).then_inc(s_ya, 1)

                def chunk_stats(c):
                    dve.wait_ge(s_xn[c % 2], c // 2 + 1)
                    for e in range(GX):
                        last = stats(c * GX + e)
                    last.then_inc(s_bn2, 1)

                for c in range(AHEAD):
                    scale(c)
                for c in range(NXC):
                    if c + AHEAD < NXC:
                        scale(c + AHEAD)
                    if c % 2 == 0:
                        dve.wait_ge(s_yc, c + 1)
                        v.tensor_tensor(xc(c), xc(c), yc(c), ALU.add).then_inc(s_xn[0], 1)
                    if c >= 1:
                        chunk_stats(c - 1)
                chunk_stats(NXC - 1)
                dve.wait_ge(s_bn2, NXC)
                layernorm_scales(dve, 4)

            @block.scalar
            def _(act):
                act.activation(ss[:, :], ss[:, :], ACT.Sqrt).then_inc(s_nrm, 1)
                for c in range(NXC):
                    act.wait_ge(s_d[c % 2], c // 2 + 1)
                    if c >= 2:
                        act.wait_ge(s_dms, c - 1)
                    act.activation(tmp[:, 2 + c % 2, :], yc(c), ACT.Square).then_inc(s_dq, 1)
                act.wait_ge(s_vb, 5)
                act.activation(stat[:, 4, :], stat[:, 3, :], ACT.Sqrt, bias=eps_col[:, 0:1]).then_inc(s_var, 1)
                for c in range(NXC):
                    act.wait_ge(s_yb, c + 1)
                    for b in range(c * GX, (c + 1) * GX):
                        yb = y[:, b * F:(b + 1) * F]
                        last = act.activation(yb, yb, ACT.Relu, scale=nm[:, b:b + 1])
                    last.then_inc(s_yc, 1)
                layernorm_std(act, 4)

            @block.gpsimd
            def _(pool):
                g = nc.gpsimd
                g.memset(block_mask, 1.0).then_inc(s_cutmask, 1)
                pool.wait_ge(s_cutmask, 1)
                g.affine_select(out=block_mask, in_=block_mask, compare_op=ALU.is_ge, fill=0.0,
                                base=0, pattern=[[1, XC]], channel_multiplier=-F).then_inc(s_cutmask, 1)
                pool.wait_ge(s_cutmask, 2)
                g.affine_select(out=block_mask, in_=block_mask, compare_op=ALU.is_ge, fill=0.0,
                                base=F - 1, pattern=[[-1, XC]], channel_multiplier=F).then_inc(s_cutmask, 1)
                pool.wait_ge(s_vb, 2)
                normalise(pool, g, 1)
                pool.wait_ge(s_mean, 1)
                centre(pool, g, 1)

                def shift_chunk(c):
                    pool.wait_ge(s_ya, c + 1)
                    g.tensor_tensor(g3(yc(c)), g3(yc(c)), per_feature(beta[:, :]), ALU.add).then_inc(s_yb, 1)

                for c in range(AHEAD):
                    shift_chunk(c)
                for c in range(NXC):
                    if c + AHEAD < NXC:
                        shift_chunk(c + AHEAD)
                    if c % 2 == 1:
                        pool.wait_ge(s_yc, c + 1)
                        g.tensor_tensor(xc(c), xc(c), yc(c), ALU.add).then_inc(s_xn[1], 1)

        s_hn3 = [sem(f"l3_h_normalised{u}") for u in range(2)]
        s_p3 = [sem(f"l3_stage_done{u}") for u in range(2)]
        s_c3 = [sem(f"l3_stage_copied{u}") for u in range(2)]
        s_out = [sem(f"stored{u}") for u in range(2)]

        with nc.Block() as block:
            @block.tensor
            def _(pe):
                with pe.Fori(0, NI) as i:
                    for st in range(3):
                        for u in range(2):
                            ps = bank[4 * u + st]
                            b0 = GS * grp(u, i)
                            if st > 0:
                                pe.wait_ge(s_c3[u], 3 * i + st)
                            if st == 0:
                                pe.wait_ge(s_hn3[u], i + 1)
                                for q in range(GS):
                                    cols = slice(q * N, (q + 1) * N)
                                    hq = hn[:, u, (q + 1) * F:(q + 2) * F]
                                    nc.tensor.matmul(ps[:, cols], hn[:, u, q * F:(q + 2) * F],
                                                     adjT[:, ds((b0 + q) * N, N)], start=True, stop=True)
                                    last = nc.tensor.transpose(ps[0:F, cols], hq, ident[:, :])
                            elif st == 1:
                                last = nc.tensor.matmul(ps[0:F, :], l3w1[:, :], msg[:, u, :], start=True, stop=True)
                            else:
                                for q in range(GS):
                                    cols = slice(q * N, (q + 1) * N)
                                    last = nc.tensor.matmul(ps[:, q * F:(q + 1) * F], hT[:, u, cols], l3w2[:, :],
                                                            start=True, stop=True)
                            last.then_inc(s_p3[u], 1)

            @block.scalar
            def _(act):
                nc.scalar.activation(std[:, 0:1], eps_col[:, 0:1], ACT.Tanh)
                act.wait_ge(s_ln, 4)
                for u in range(2):
                    for q in range(GS):
                        norm_graph(s_hn3[u], u, GS * u, q, q == GS - 1)

                def group_pair(i, more):
                    for u in range(2):
                        act.wait_ge(s_p3[u], 3 * i + 2)
                        nc.scalar.activation(hT[0:F, u, :], bank[4 * u + 1][0:F, :], ACT.Tanh, bias=l3b1[:, 0:1])\
                          .then_inc(s_c3[u], 1)
                        if more:
                            for v, q in ((0, 0),) if u == 0 else ((0, 1), (0, 2), (0, 3), (1, 0), (1, 1), (1, 2), (1, 3)):
                                norm_graph(s_hn3[v], v, GS * grp(v, i + 1), q, q == GS - 1)

                with act.Fori(0, NI - 1) as i:
                    group_pair(i, True)
                group_pair(NI - 1, False)

            @block.vector
            def _(dve):
                with dve.Fori(0, NI) as i:
                    for u in range(2):
                        dve.wait_ge(s_p3[u], 3 * i + 1)
                        nc.vector.tensor_copy(msg[:, u, :], bank[4 * u][:, :]).then_inc(s_c3[u], 1)
                    for u in range(2):
                        dve.wait_ge(s_p3[u], 3 * i + 3)
                        dve.wait_ge(s_out[u], 16 * i)
                        nc.vector.tensor_tensor(upd[:, u, :], bank[4 * u + 2][:, 0:GS * F],
                                                x[:, ds(GS * grp(u, i) * F, GS * F)], ALU.add).then_inc(s_c3[u], 1)

            @block.sync
            def _(sp):
                with sp.Fori(0, NI) as i:
                    for u in range(2):
                        sp.wait_ge(s_c3[u], 3 * i + 3)
                        sp.dma_start(out_v[:, ds(GS * grp(u, i), GS), :],
                                     upd[:, u, :].rearrange("p (q f) -> p q f", q=GS)).then_inc(s_out[u], 16)
                for u in range(2):
                    sp.wait_ge(s_out[u], 16 * NI)


_INS = ["x", "adj", "nodemask", "L0_gnn_W1", "L0_gnn_b1", "L0_gnn_W2", "L0_gnn_b2",
        "L1_gnn_W0", "L1_gnn_b0", "L1_gnn_W1", "L1_gnn_b1", "L1_gnn_W2", "L1_gnn_b2",
        "L1_gnn_Wout", "L1_gnn_bout", "L2_gnn_weight", "L2_gnn_bias", "L2_gnn_gamma",
        "L2_gnn_beta", "L3_gnn_W1", "L3_gnn_b1", "L3_gnn_W2", "L3_gnn_b2"]
_OUTS = [((128, 128, 64), "float32")]


def kernel(**inputs):
    import numpy as _np
    import concourse.bacc as _bacc
    from concourse import mybir as _mybir
    from concourse.bass_utils import run_bass_kernel_spmd as _run

    nc = _bacc.Bacc("TRN2", target_bir_lowering=False, num_devices=1)
    arrays, args = {}, {}
    for name in _INS:
        v = _np.ascontiguousarray(inputs[name])
        arrays[f"in_{name}_dram"] = v
        args[name] = nc.dram_tensor(f"in_{name}_dram", v.shape, _mybir.dt.from_np(v.dtype), kind="ExternalInput").ap()
    outs = [nc.dram_tensor(f"out_{i}_dram", s, _mybir.dt.from_np(_np.dtype(d)), kind="ExternalOutput").ap()
            for i, (s, d) in enumerate(_OUTS)]
    gnn_stack_kernel(nc, args, outs[0])
    r = _run(nc, [arrays], core_ids=[0])
    return r.results[0]["out_0_dram"]
```
